# Optimizing a Trainium2 kernel written in Bass

```python
import numpy as np
import jax
import jax.numpy as jnp

def _softmax(x, axis=-1):
    return jax.nn.softmax(x, axis=axis)

def _gelu(x):
    return jax.nn.gelu(x, approximate=True)

def _silu(x):
    return jax.nn.silu(x)

def _sigmoid(x):
    return jax.nn.sigmoid(x)

def _layernorm(x, axis=-1, eps=1e-05):
    m = jnp.mean(x, axis=axis, keepdims=True)
    v = jnp.var(x, axis=axis, keepdims=True)
    return (x - m) / jnp.sqrt(v + eps)

def _scatter_add(tgt, idx, src, axis=0):
    return tgt.at[idx].add(src)

def _segment_sum(src, seg, n):
    return jax.ops.segment_sum(src, seg, n)
kernel_name = 'mk_flamingo_gated_d1_seqx_r4_98ec34'

def setup_inputs(seed: int=0):
    np.random.seed(seed)
    _w = jnp.asarray

    def _rec_inputs():
        import jax
        import jax.numpy as jnp
        _rk = jax.random.key(seed)
        x = 0.5 + 0.2887 * jax.random.normal(jax.random.fold_in(_rk, 1), (4, 512, 512), jnp.float32)
        _lenS = 512 - jax.random.randint(jax.random.fold_in(_rk, 7), (4,), 0, max(1, 512 // 4) + 1, jnp.int32)
        _lenS2 = 512 - jax.random.randint(jax.random.fold_in(_rk, 8), (4,), 0, max(1, 512 // 4) + 1, jnp.int32)
        _ctx_512P = jax.random.normal(jax.random.fold_in(_rk, 11), (4, 16, 128), jnp.float32)
        _ctx_512c = jax.random.dirichlet(jax.random.fold_in(_rk, 511), 0.3 * jnp.ones((16,), jnp.float32), (4, 512))
        _ctx_512t = jnp.einsum('bsk,bkd->bsd', _ctx_512c, _ctx_512P)
        _ctx_512t = _ctx_512t * jax.lax.rsqrt(jnp.mean(jnp.square(_ctx_512t)) + 1e-12) * 0.953939
        ctx_512 = -0.000392918 + 0.999932 * (_ctx_512t + 0.3 * jax.random.normal(jax.random.fold_in(_rk, 611), (4, 512, 128), jnp.float32))
        _g = jax.random.normal(jax.random.fold_in(_rk, 9001), (2, 1), jnp.float32)
        _g = jnp.sign(_g) * jnp.maximum(jnp.abs(_g), 1.0) + (_g == 0) * 1.0
        g_xattn = _g[0]
        g_ffn = _g[1]
        return (x, ctx_512, g_xattn, g_ffn)
    x, ctx_512, g_xattn, g_ffn = _rec_inputs()

    def _L0_xattn_setup():
        import jax, jax.numpy as jnp
        import numpy as np
        B, N, D = (16, 512, 128)
        H = 4
        TOP_K_RATIO = 0.3
        key = jax.random.key(seed)
        k1, k2, k3, k4 = jax.random.split(key, 4)
        h = jax.random.normal(k1, (B, N, D), dtype=jnp.float32)
        adj_raw = jax.random.uniform(k2, (B, N, N), dtype=jnp.float32)
        lim = 1.0 / np.sqrt(D)
        Wq = jax.random.uniform(k3, (D, D), minval=-lim, maxval=lim, dtype=jnp.float32)
        Wk = jax.random.uniform(k4, (D, D), minval=-lim, maxval=lim, dtype=jnp.float32)
        gamma_raw = jnp.float32(-0.85)
        return {'h': h, 'adj_raw': adj_raw, 'Wq': Wq, 'Wk': Wk, 'gamma_raw': gamma_raw}
    _L0_xattn_all = _L0_xattn_setup()
    _L0_xattn_in = {k: v for k, v in _L0_xattn_all.items() if k in ('Wq', 'Wk', 'gamma_raw')}
    del _L0_xattn_all

    def _L0_ffn_setup():
        import jax, jax.numpy as jnp
        import numpy as np
        B, S, D, I, E, K = (4, 256, 512, 256, 8, 2)
        key = jax.random.key(seed)
        ks = jax.random.split(key, 7)

        def w(k, shape, fan_in):
            return jax.random.normal(k, shape, dtype=jnp.float32) * fan_in ** (-0.5)
        return {'hidden_states': jax.random.normal(ks[0], (B, S, D), dtype=jnp.float32), 'router_w': w(ks[1], (D, E), D), 'gate_up_w': w(ks[2], (E, D, 2 * I), D), 'down_w': w(ks[3], (E, I, D), I), 'shared_gate_w': w(ks[4], (D, I), D), 'shared_up_w': w(ks[5], (D, I), D), 'shared_down_w': w(ks[6], (I, D), I)}
    _L0_ffn_all = _L0_ffn_setup()
    _L0_ffn_in = {k: v for k, v in _L0_ffn_all.items() if k in ('router_w', 'gate_up_w', 'down_w', 'shared_gate_w', 'shared_up_w', 'shared_down_w')}
    del _L0_ffn_all
    return {'x': x, 'ctx_512': ctx_512, 'g_xattn': g_xattn, 'g_ffn': g_ffn, 'L0_xattn_Wq': _L0_xattn_in['Wq'], 'L0_xattn_Wk': _L0_xattn_in['Wk'], 'L0_xattn_gamma_raw': _L0_xattn_in['gamma_raw'], 'L0_ffn_router_w': _L0_ffn_in['router_w'], 'L0_ffn_gate_up_w': _L0_ffn_in['gate_up_w'], 'L0_ffn_down_w': _L0_ffn_in['down_w'], 'L0_ffn_shared_gate_w': _L0_ffn_in['shared_gate_w'], 'L0_ffn_shared_up_w': _L0_ffn_in['shared_up_w'], 'L0_ffn_shared_down_w': _L0_ffn_in['shared_down_w']}

def reference(x, ctx_512, g_xattn, g_ffn, L0_xattn_Wq, L0_xattn_Wk, L0_xattn_gamma_raw, L0_ffn_router_w, L0_ffn_gate_up_w, L0_ffn_down_w, L0_ffn_shared_gate_w, L0_ffn_shared_up_w, L0_ffn_shared_down_w):
    import jax
    import jax.numpy as jnp

    def _L0_xattn_ref(h, adj_raw, Wq, Wk, gamma_raw):
        import jax, jax.numpy as jnp
        import numpy as np
        B, N, D = (16, 512, 128)
        H = 4
        TOP_K_RATIO = 0.3
        b, n, dm = h.shape
        d = dm // H
        Q = (h @ Wq.T).reshape(b, n, H, d).transpose(0, 2, 1, 3)
        K = (h @ Wk.T).reshape(b, n, H, d).transpose(0, 2, 1, 3)
        sim = jnp.einsum('bhnd,bhmd->bnm', Q, K) / (jnp.sqrt(jnp.float32(d)) * H)
        k = max(1, int(n * TOP_K_RATIO))
        topk_vals = jax.lax.top_k(sim, k)[0]
        threshold = topk_vals[:, :, -1:]
        sparse_mask = (sim >= threshold).astype(sim.dtype)
        A_learned = jax.nn.sigmoid(sim) * sparse_mask
        A_learned = (A_learned + jnp.swapaxes(A_learned, -1, -2)) * 0.5
        gamma = jax.nn.sigmoid(gamma_raw)
        return (1.0 - gamma) * adj_raw + gamma * A_learned

    def _L0_ffn_ref(hidden_states, router_w, gate_up_w, down_w, shared_gate_w, shared_up_w, shared_down_w):
        import jax, jax.numpy as jnp
        import numpy as np
        B, S, D, I, E, K = (4, 256, 512, 256, 8, 2)
        Bb, Ss, Dd = hidden_states.shape
        x = hidden_states.reshape(-1, Dd)
        T = x.shape[0]
        shared = jax.nn.silu(x @ shared_gate_w) * (x @ shared_up_w) @ shared_down_w
        logits = x @ router_w
        top_val, top_idx = jax.lax.top_k(logits, K)
        probs = jnp.zeros_like(logits).at[jnp.arange(T)[:, None], top_idx].set(jax.nn.sigmoid(top_val))
        xin = probs.T[:, :, None] * x[None]
        gu = jnp.einsum('etd,edf->etf', xin, gate_up_w)
        gate, up = jnp.split(gu, 2, axis=-1)
        h = jax.nn.silu(gate) * up
        expert_out = jnp.einsum('eti,eid->etd', h, down_w)
        combined = shared + expert_out.sum(axis=0)
        return combined.reshape(Bb, Ss, Dd)
    x = x + jnp.tanh(g_xattn[0]) * _L0_xattn_ref(ctx_512, _layernorm(x, axis=-1), L0_xattn_Wq, L0_xattn_Wk, L0_xattn_gamma_raw)
    x = x + jnp.tanh(g_ffn[0]) * _L0_ffn_ref(_layernorm(x, axis=-1), L0_ffn_router_w, L0_ffn_gate_up_w, L0_ffn_down_w, L0_ffn_shared_gate_w, L0_ffn_shared_up_w, L0_ffn_shared_down_w)
    return x

_drawn_inputs = setup_inputs


def setup_inputs(seed=0):
    import zlib

    import numpy as np

    out = dict(_drawn_inputs(seed))
    spreads = {}
    factors = {}
    for name, (base, spread) in spreads.items():
        noise = np.random.default_rng([zlib.crc32(name.encode()), seed]).standard_normal(out[name].shape)
        drawn = base * np.exp(spread * noise) if base else spread * noise
        out[name] = jnp.asarray(drawn.astype(out[name].dtype))
    for name, factor in factors.items():
        out[name] = (out[name] * factor).astype(out[name].dtype)
    return out
```

```python
from contextlib import ExitStack

import concourse.bass as bass
from concourse import mybir

F32 = mybir.dt.float32
BF16 = mybir.dt.bfloat16
I32 = mybir.dt.int32
U32 = mybir.dt.uint32
U8 = mybir.dt.uint8
ALU = mybir.AluOpType
ACT = mybir.ActivationFunctionType
AX_X = mybir.AxisListType.X

P = 128
EPS = 1e-5
TOP_K_RATIO = 0.3
HEADS = 4
BIG = 1e30
COUNTS = 5
Z_START = 0.52


def flamingo_gated_block(nc, x, ctx_in, g_xattn, g_ffn, wq, wk, gamma_raw, router_w, gate_up_w, down_w,
                         sh_gate_w, sh_up_w, sh_down_w, out):
    B, N, D = x.shape
    C = ctx_in.shape[2]
    E, _, F2 = gate_up_w.shape
    I = F2 // 2
    T = B * N
    RT = N // P
    DC = D // P
    IC = I // P
    CAP = T // P
    COLS = E * CAP
    MT = 2 * T // P + E - 1
    ROW = D + E
    SCALE = 1.0 / (float(C // HEADS) ** 0.5 * HEADS)
    KTH = max(1, int(N * TOP_K_RATIO))
    WIN = 8
    AIM = KTH - WIN / 2 - 0.5
    DENS = N * 0.348
    assert C == P and N == D == 512 and COLS == P and F2 == 512 and RT == 4

    x2_rows = nc.dram_tensor("x2_rows", (T + P, ROW), F32).ap()

    with ExitStack() as stack:
        def sb(name, shape, dt=F32):
            return stack.enter_context(nc.sbuf_tensor(name, shape, dt))

        def sem(name):
            return stack.enter_context(nc.semaphore(name))

        w_gu = sb("w_gu", [P, E * DC * F2])
        w_dn = sb("w_dn", [P, E * IC * D])
        w_shgu = sb("w_shgu", [P, DC, F2])
        w_shdn = sb("w_shdn", [P, IC, D])
        w_rt = sb("w_rt", [P, DC, E])
        wqkT = sb("wqkT", [P, 2, C])
        ctx_sb = sb("ctx_sb", [P, RT, C])
        ctxT = sb("ctxT", [P, N])
        qT = sb("qT", [P, N])
        kT = sb("kT", [P, N])
        sim = sb("sim", [P, 2, RT, N])
        adj = sb("adj", [P, 2, RT, N])
        ge = sb("ge", [P, RT, N], U8)
        tmp = sb("tmp", [P, 2, N])
        xs = sb("xs", [P, 2, RT, D])
        x2 = sb("x2", [P, RT, ROW])
        x2T = sb("x2T", [P, RT, DC, P])
        silu = sb("silu", [P, 2, I])
        h = sb("h", [P, 2, I])
        hT = sb("hT", [P, 2, IC, P])
        scal = sb("scal", [1, 4])
        scal_t = sb("scal_t", [1, 4])
        gates = sb("gates", [P, 4])
        c12 = sb("c12", [P, 4])
        simsum = sb("simsum", [P, 2, RT])
        simsq = sb("simsq", [P, 2, RT])
        mean = sb("mean", [P, RT])
        msq = sb("msq", [P, RT])
        powin = sb("powin", [P, 2, RT])
        powexp = sb("powexp", [P, 2, RT])
        powout = sb("powout", [P, 2, RT])
        pow2in = sb("pow2in", [P, RT])
        pow2out = sb("pow2out", [P, RT])
        stats = sb("stats", [P, RT, 6])
        mv = sb("mv", [P, RT, 2])
        xmul = sb("xmul", [P, RT])
        xadd = sb("xadd", [P, RT])
        x2add = sb("x2add", [P, RT])
        slope = sb("slope", [P, 3, RT])
        probe = sb("probe", [P, COUNTS, RT])
        cnt = sb("cnt", [P, COUNTS, RT])
        u = sb("u", [P, 8, RT])
        top8 = sb("top8", [P, RT, 8])
        sel8 = sb("sel8", [P, RT, 8])
        thr = sb("thr", [P, RT])
        bad = sb("bad", [P, 1], BF16)
        bad_i = sb("bad_i", [1, 1], I32)
        logit = sb("logit", [P, RT, E])
        v8 = sb("v8", [P, RT, 8])
        i8 = sb("i8", [P, RT, 8], U32)
        prob = sb("prob", [P, RT, 2])
        ef = sb("ef", [P, 2, RT])
        oh = sb("oh", [P, 2, RT, E])
        ohp = sb("ohp", [P, 2, RT, E])
        mask = sb("mask", [P, RT, E], BF16)
        msum = sb("msum", [P, E], BF16)
        mred = sb("mred", [P, E])
        rsel = sb("rsel", [P, 2, RT, E])
        rank = sb("rank", [P, 2 * RT])
        rank_i = sb("rank_i", [P, 3, 2 * RT], I32)
        rank_f = sb("rank_f", [P, 2, 2 * RT])
        col = sb("col", [P, 2 * RT])
        delta = sb("delta", [P, 2 * RT])
        oh_slot = sb("oh_slot", [P, 2 * RT, P], BF16)
        oh_col = sb("oh_col", [P, 2 * RT, 2, COLS], BF16)
        table = sb("table", [P, 2, COLS])
        n_e = sb("n_e", [E, 2], I32)
        tiles_e = sb("tiles_e", [E, 2])
        tile_pos = sb("tile_pos", [P, 4])
        idx = sb("idx", [P, MT], I32)
        etab = sb("etab", [1, MT], I32)
        p_t = sb("p_t", [P, 2])
        p_junk = sb("p_junk", [P, 2, E])
        ident = sb("ident", [P, P])
        upper = sb("upper", [P, P], BF16)
        ones = sb("ones", [P, P], BF16)
        ones_f = sb("ones_f", [P, P])
        iota_b = sb("iota_b", [P, P], BF16)
        iota8 = sb("iota8", [P, 8])
        iota_m = sb("iota_m", [P, MT])
        part = sb("part", [P, 1])
        e_of = sb("e_of", [P, P])
        r_of = sb("r_of", [P, 1])
        e_lt = sb("e_lt", [E, COLS])
        e_eq = sb("e_eq", [E, COLS])
        part_i = sb("part_i", [P, 3], I32)

        bank = [stack.enter_context(nc.psum_tensor(f"bank{n}", [P, 512], F32)) for n in range(8)]
        b_small, b_y, b_sim, b_t, b_gu = bank[0], bank[1], bank[2:4], bank[4:6], bank[6:8]
        ps_logit = b_small[:, 0:RT * E]
        ps_rank = b_small[:, 32:32 + RT * E]
        ps_bad = b_small[0:1, 64:65]
        ps_table = b_small[:, 256:512]
        xg, xgT, y_sb = x2, x2T, tmp
        wqk = tmp[:, :, 0:C]
        late = adj[:, 0, :, :].rearrange("p i n -> p (i n)")
        table_t = late[:, 0:COLS]
        place = late[:, COLS:COLS + MT]
        oh_e = late[:, 512:512 + MT * E].rearrange("p (t e) -> p t e", e=E)
        zeros = x2[:, 0]

        ctx_loaded = sem("ctx_loaded")
        x_in = [sem("x_in_even"), sem("x_in_odd")]
        wqk_in = sem("wqk_in")
        scal_in = sem("scal_in")
        shw_in = sem("shw_in")
        rtw_in = sem("rtw_in")
        exw_in = sem("exw_in")
        pool_step = sem("pool_step")
        const_ready = sem("const_ready")
        zero_ready = sem("zero_ready")
        scal_ready = sem("scal_ready")
        gates_bc = sem("gates_bc")
        gates_ready = sem("gates_ready")
        wT_ps = sem("wT_ps")
        wT_ready = sem("wT_ready")
        s1_ps = sem("s1_ps")
        s1_done = sem("s1_done")
        pow_in = sem("pow_in")
        pow_out = sem("pow_out")
        affine_in = sem("affine_in")
        affine_out = sem("affine_out")
        bad_in = sem("bad_in")
        bad_ps = sem("bad_ps")
        masked = sem("masked")
        at_ps = sem("at_ps")
        at_used = sem("at_used")
        pow2_in = sem("pow2_in")
        pow2_out = sem("pow2_out")
        x2_in = sem("x2_in")
        x2_ready = sem("x2_ready")
        x2t_ps = sem("x2t_ps")
        x2t_done = sem("x2t_done")
        logit_ps = sem("logit_ps")
        logit_used = sem("logit_used")
        top2 = sem("top2")
        prob_ready = sem("prob_ready")
        mask_ready = sem("mask_ready")
        msum_ready = sem("msum_ready")
        rank_ps = sem("rank_ps")
        payload = sem("payload")
        slot_oh = sem("slot_oh")
        table_ps = sem("table_ps")
        table_used = sem("table_used")
        fin_v = sem("fin_v")
        fin_t = sem("fin_t")
        gu_ps = sem("gu_ps")
        silu_ready = sem("silu_ready")
        h_ready = sem("h_ready")
        ht_ps = sem("ht_ps")
        ht_done = sem("ht_done")
        y_ps = sem("y_ps")
        base_ready = sem("base_ready")
        rows_out = sem("rows_out")
        base_out = sem("base_out")
        dummy_out = sem("dummy_out")
        gathered = [sem("gathered_even"), sem("gathered_odd")]
        scattered = sem("scattered")
        m_xt_ps = sem("m_xt_ps")
        m_xt = sem("m_xt")
        m_gu_ps = sem("m_gu_ps")
        m_p = sem("m_p")
        m_silu = sem("m_silu")
        m_h = sem("m_h")
        m_ht_ps = sem("m_ht_ps")
        m_ht = sem("m_ht")
        m_y_ps = sem("m_y_ps")
        m_y = sem("m_y")
        vector_step = sem("vector_step")
        scalar_step = sem("scalar_step")

        x_v = x.rearrange("b (i p) d -> b p i d", p=P)
        ctx_v = ctx_in.rearrange("b (i p) d -> b p i d", p=P)
        out_v = out[0:T, :].rearrange("(b i p) d -> b p i d", p=P, i=RT)
        rows_v = x2_rows[0:T, :].rearrange("(b i p) d -> b p i d", p=P, i=RT)

        block = stack.enter_context(nc.Block())

        @block.sync
        def _(sp):
            def load_ctx(b):
                sp.wait_ge(s1_ps, 7 * (b - 1) + 1)
                sp.dma_start(ctx_sb[:, :, :], ctx_v[b]).then_inc(ctx_loaded, 16)

            def load_x(b):
                if b >= 2:
                    sp.wait_ge(base_out, 16 * (b - 1))
                sp.dma_start(xs[:, b % 2], x_v[b]).then_inc(x_in[b % 2], 16)

            sp.dma_start(ctx_sb[:, :, :], ctx_v[0]).then_inc(ctx_loaded, 16)
            sp.dma_start(wqk[:, 0], wq).then_inc(wqk_in, 16)
            sp.dma_start(wqk[:, 1], wk).then_inc(wqk_in, 16)
            for n, g in enumerate((g_xattn, g_ffn, gamma_raw)):
                sp.dma_start(scal[0:1, n:n + 1], g).then_inc(scal_in, 16)
            load_x(0)
            load_ctx(1)
            load_x(1)
            sp.dma_start(w_rt[:, :, :], router_w.rearrange("(c p) e -> p c e", p=P)).then_inc(rtw_in, 16)
            sp.dma_start(w_shgu[:, :, 0:I], sh_gate_w.rearrange("(c p) f -> p c f", p=P)).then_inc(shw_in, 16)
            sp.dma_start(w_shgu[:, :, I:F2], sh_up_w.rearrange("(c p) f -> p c f", p=P)).then_inc(shw_in, 16)
            sp.dma_start(w_shdn[:, :, :], sh_down_w.rearrange("(c p) d -> p c d", p=P)).then_inc(shw_in, 16)
            sp.wait_ge(zero_ready, 1)
            sp.dma_start(x2_rows[T:T + P, :], zeros).then_inc(dummy_out, 16)
            sp.dma_start(out[T:T + P, :], x2[:, 0, 0:D]).then_inc(dummy_out, 16)
            for e in range(E):
                sp.dma_start(w_gu[:, e * DC * F2:(e + 1) * DC * F2].rearrange("p (c f) -> p c f", c=DC),
                             gate_up_w[e].rearrange("(c p) f -> p c f", p=P)).then_inc(exw_in, 16)
                sp.dma_start(w_dn[:, e * IC * D:(e + 1) * IC * D].rearrange("p (c d) -> p c d", c=IC),
                             down_w[e].rearrange("(c p) d -> p c d", p=P)).then_inc(exw_in, 16)
            for b in range(B):
                if b + 2 < B:
                    load_ctx(b + 2)
                sp.wait_ge(x2_ready, RT * (b + 1))
                sp.wait_ge(payload, b + 1)
                sp.dma_start(rows_v[b], x2[:, :, :]).then_inc(rows_out, 16)
                sp.wait_ge(base_ready, RT * (b + 1))
                sp.dma_start(out_v[b], xs[:, b % 2]).then_inc(base_out, 16)
                if b + 2 < B:
                    load_x(b + 2)
            sp.wait_ge(rows_out, 16 * B)
            sp.wait_ge(base_out, 16 * B)
            sp.wait_ge(dummy_out, 32)
            sp.wait_ge(scattered, 16 * MT)

        @block.gpsimd
        def _(pool):
            steps = [0]

            def link(ins):
                steps[0] += 1
                ins.then_inc(pool_step, 1)
                pool.wait_ge(pool_step, steps[0])

            nc.gpsimd.memset(zeros, 0.0).then_inc(zero_ready, 1)
            nc.gpsimd.memset(ones[:, :], 1.0)
            nc.gpsimd.memset(ones_f[:, :], 1.0)
            nc.gpsimd.memset(e_lt[:, :], 1.0)
            nc.gpsimd.memset(e_eq[:, :], 1.0)
            nc.gpsimd.memset(msum[:, :], 0.0)
            nc.gpsimd.memset(powexp[:, 0], 0.5)
            link(nc.gpsimd.memset(powexp[:, 1], -0.5))
            nc.gpsimd.affine_select(out=ident[:, :], in_=ones_f[:, :], compare_op=ALU.is_equal, fill=0.0, base=0,
                                    pattern=[[-1, P]], channel_multiplier=1)
            nc.gpsimd.affine_select(out=upper[:, :], in_=ones[:, :], compare_op=ALU.is_gt, fill=0.0, base=0,
                                    pattern=[[1, P]], channel_multiplier=-1)
            nc.gpsimd.affine_select(out=e_lt[:, :], in_=e_lt[:, :], compare_op=ALU.is_ge, fill=0.0, base=-CAP,
                                    pattern=[[1, COLS]], channel_multiplier=-CAP)
            link(nc.gpsimd.affine_select(out=e_eq[:, :], in_=e_eq[:, :], compare_op=ALU.is_ge, fill=0.0, base=0,
                                         pattern=[[1, COLS]], channel_multiplier=-CAP))
            nc.gpsimd.affine_select(out=e_eq[:, :], in_=e_eq[:, :], compare_op=ALU.is_ge, fill=0.0, base=CAP - 1,
                                    pattern=[[-1, COLS]], channel_multiplier=CAP)
            nc.gpsimd.iota(iota_b[:, :], [[1, P]], base=0, channel_multiplier=0, allow_small_or_imprecise_dtypes=True)
            nc.gpsimd.iota(iota8[:, :], [[1, 8]], base=0, channel_multiplier=0, allow_small_or_imprecise_dtypes=True)
            nc.gpsimd.iota(iota_m[:, :], [[1, MT]], base=0, channel_multiplier=0, allow_small_or_imprecise_dtypes=True)
            nc.gpsimd.iota(part[:, :], [[0, 1]], base=0, channel_multiplier=1, allow_small_or_imprecise_dtypes=True)
            nc.gpsimd.iota(part_i[:, 0:1], [[0, 1]], base=0, channel_multiplier=1).then_inc(const_ready, 1)

            for b in range(B):
                pool.wait_ge(pow_in, b + 1)
                nc.gpsimd.tensor_tensor(powout[:, :, :], powin[:, :, :], powexp[:, :, :], ALU.pow).then_inc(pow_out, 1)
                pool.wait_ge(affine_in, b + 1)
                for i in range(RT):
                    nc.gpsimd.tensor_scalar(xs[:, b % 2, i], xs[:, b % 2, i], xmul[:, i:i + 1], xadd[:, i:i + 1],
                                            ALU.mult, ALU.add).then_inc(affine_out, 1)
                pool.wait_ge(pow2_in, b + 1)
                nc.gpsimd.tensor_tensor(pow2out[:, :], pow2in[:, :], powexp[:, 1], ALU.pow).then_inc(pow2_out, 1)

            pool.wait_ge(fin_v, FIN_V_IDX)
            pool.wait_ge(dummy_out, 32)

            def gather(t):
                nc.gpsimd.indirect_dma_start(out=xg[:, t % 2, :], out_offset=None, in_=x2_rows[:, :],
                                             in_offset=bass.IndirectOffsetOnAxis(ap=idx[:, t:t + 1], axis=0)
                                             ).then_inc(gathered[t % 2], 16)

            def scatter(t):
                nc.gpsimd.indirect_dma_start(out=out[:, :],
                                             out_offset=bass.IndirectOffsetOnAxis(ap=idx[:, t:t + 1], axis=0),
                                             in_=y_sb[:, t % 2, :], in_offset=None, compute_op=ALU.add
                                             ).then_inc(scattered, 16)

            pool.wait_ge(rows_out, 16 * B)
            gather(0)
            gather(1)
            pool.wait_ge(base_out, 16 * B)
            for t in range(MT):
                if t + 2 < MT:
                    pool.wait_ge(m_xt_ps, t + 1)
                    pool.wait_ge(m_p, t + 1)
                    gather(t + 2)
                if t:
                    if t >= 2:
                        pool.wait_ge(scattered, 16 * (t - 1))
                    pool.wait_ge(m_y, t)
                    scatter(t - 1)
            pool.wait_ge(scattered, 16 * (MT - 1))
            pool.wait_ge(m_y, MT)
            scatter(MT - 1)

        @block.scalar
        def _(act):
            act.wait_ge(scal_in, 48)
            nc.scalar.activation(scal_t[0:1, 0:2], scal[0:1, 0:2], ACT.Tanh)
            nc.scalar.activation(scal_t[0:1, 2:3], scal[0:1, 2:3], ACT.Sigmoid).then_inc(scal_ready, 1)
            act.wait_ge(wT_ps, 1)
            nc.scalar.copy(wqkT[:, :, :], b_t[0][:, 0:2 * C].rearrange("p (a c) -> p a c", a=2)).then_inc(wT_ready, 1)

            def stage1(b):
                q = b % 2
                for j, dst in enumerate((ctxT, qT, kT)):
                    act.wait_ge(s1_ps, 7 * b + j + 1)
                    nc.scalar.copy(dst[:, :], b_sim[j % 2][:, :]).then_inc(s1_done, 1)
                for i in range(RT):
                    ps = b_sim[(3 + i) % 2]
                    act.wait_ge(s1_ps, 7 * b + i + 4)
                    if b >= 2 and i == 0:
                        act.wait_ge(masked, RT * (b - 1))
                        act.wait_ge(at_ps, RT * (b - 1))
                        act.wait_ge(at_used, RT * (b - 1))
                    nc.scalar.activation(sim[:, q, i], ps[:, :], ACT.Copy, accum_out=simsum[:, q, i:i + 1])
                    nc.scalar.activation(adj[:, q, i], ps[:, :], ACT.Square,
                                         accum_out=simsq[:, q, i:i + 1]).then_inc(scalar_step, 1)
                    act.wait_ge(scalar_step, RT * b + i + 1)
                    nc.scalar.activation(adj[:, q, i], ps[:, :], ACT.Sigmoid, scale=SCALE).then_inc(s1_done, 1)

            stage1(0)
            stage1(1)
            act.wait_ge(gates_bc, 1)
            nc.scalar.copy(gates[:, 0:3], b_small[:, 0:3]).then_inc(gates_ready, 1)
            for b in range(B):
                act.wait_ge(x2_in, b + 1)
                if b:
                    act.wait_ge(rows_out, 16 * b)
                else:
                    act.wait_ge(dummy_out, 32)
                for i in range(RT):
                    nc.scalar.activation(x2[:, i, 0:D], xs[:, b % 2, i], ACT.Identity, scale=pow2out[:, i:i + 1],
                                         bias=x2add[:, i:i + 1]).then_inc(x2_ready, 1)
                for i in range(RT):
                    act.wait_ge(x2t_ps, RT * b + i + 1)
                    if b and i == 0:
                        act.wait_ge(gu_ps, RT * b)
                    nc.scalar.copy(x2T[:, i], b_t[i % 2][:, :].rearrange("p (c t) -> p c t", c=DC)).then_inc(x2t_done, 1)
                if b + 2 < B:
                    stage1(b + 2)
                act.wait_ge(top2, b + 1)
                if b:
                    act.wait_ge(payload, b)
                nc.scalar.activation(prob[:, :, :], v8[:, :, 0:2], ACT.Sigmoid).then_inc(prob_ready, 1)

                def silu_of(i):
                    n = RT * b + i
                    act.wait_ge(gu_ps, n + 1)
                    if n >= 2:
                        act.wait_ge(h_ready, n - 1)
                    nc.scalar.activation(silu[:, n % 2], b_gu[n % 2][:, 0:I], ACT.Silu).then_inc(silu_ready, 1)

                def ht_of(i):
                    n = RT * b + i
                    act.wait_ge(ht_ps, n + 1)
                    if n >= 2:
                        act.wait_ge(y_ps, n - 1)
                    nc.scalar.copy(hT[:, n % 2], b_sim[1][:, 0:I].rearrange("p (c t) -> p c t", c=IC)).then_inc(ht_done, 1)

                silu_of(0)
                for i in range(RT):
                    if i + 1 < RT:
                        silu_of(i + 1)
                    ht_of(i)

            def xt_out(t, par):
                act.wait_ge(m_xt_ps, t + 1)
                nc.scalar.copy(xgT[:, par], b_t[par][:, :].rearrange("p (c t) -> p c t", c=DC)).then_inc(m_xt, 1)

            def silu_out(t, par):
                act.wait_ge(m_gu_ps, t + 1)
                act.wait_ge(m_p, t + 1)
                nc.scalar.activation(silu[:, par], b_gu[par][:, 0:I], ACT.Silu, scale=p_t[:, par:par + 1]).then_inc(m_silu, 1)

            def y_out(t, par):
                act.wait_ge(m_y_ps, t + 1)
                nc.scalar.activation(y_sb[:, par], b_sim[par][:, :], ACT.Copy, scale=gates[:, 1:2]).then_inc(m_y, 1)

            act.wait_ge(gu_ps, T // P)
            xt_out(0, 0)
            xt_out(1, 1)
            act.wait_ge(h_ready, T // P)
            silu_out(0, 0)

            def step(t, par, last=False):
                if not last:
                    act.wait_ge(m_gu_ps, t)
                    xt_out(t + 1, 1 - par)
                silu_out(t, par)
                if not (isinstance(t, int) and t < 3):
                    act.wait_ge(scattered, 16 * (t - 2))
                y_out(t - 1, 1 - par)

            step(1, 1)
            step(2, 0)
            with act.Fori(3, MT - 3, 2) as t:
                step(t, 1)
                step(t + 1, 0)
            step(MT - 2, 1)
            step(MT - 1, 0, True)
            act.wait_ge(scattered, 16 * (MT - 2))
            y_out(MT - 1, 0)

        @block.tensor
        def _(pe):
            pe.wait_ge(const_ready, 1)
            pe.wait_ge(wqk_in, 32)
            nc.tensor.transpose(b_t[0][:, 0:C], wqk[:, 0], ident[:, :])
            nc.tensor.transpose(b_t[0][:, C:2 * C], wqk[:, 1], ident[:, :]).then_inc(wT_ps, 1)

            def stage1(b):
                q = b % 2
                pe.wait_ge(ctx_loaded, 16 * (b + 1))
                if b:
                    pe.wait_ge(s1_done, 7 * b)
                for j in range(RT):
                    mm = nc.tensor.transpose(b_sim[0][:, j * P:(j + 1) * P], ctx_sb[:, j], ident[:, :])
                mm.then_inc(s1_ps, 1)
                pe.wait_ge(s1_done, 7 * b + 1)
                if b == 0:
                    pe.wait_ge(wT_ready, 1)
                if b >= 3:
                    pe.wait_ge(ht_done, RT * (b - 2))
                nc.tensor.matmul(b_sim[1][:, :], wqkT[:, 0], ctxT[:, :], start=True, stop=True).then_inc(s1_ps, 1)
                nc.tensor.matmul(b_sim[0][:, :], wqkT[:, 1], ctxT[:, :], start=True, stop=True).then_inc(s1_ps, 1)
                pe.wait_ge(s1_done, 7 * b + 3)
                for i in range(RT):
                    if i >= 2:
                        pe.wait_ge(s1_done, 7 * b + i + 2)
                    nc.tensor.matmul(b_sim[(3 + i) % 2][:, :], qT[:, i * P:(i + 1) * P], kT[:, :],
                                     start=True, stop=True).then_inc(s1_ps, 1)

            def check_search(b):
                pe.wait_ge(bad_in, b + 1)
                nc.tensor.matmul(ps_bad, bad[:, :], ones[:, 0:1], start=True, stop=True).then_inc(bad_ps, 1)

            stage1(0)
            pe.wait_ge(scal_ready, 1)
            nc.tensor.matmul(b_small[:, 0:3], ones_f[0:1, :], scal_t[0:1, 0:3], start=True, stop=True).then_inc(gates_bc, 1)
            stage1(1)
            pe.wait_ge(gates_ready, 1)
            check_search(0)
            for b in range(B):
                q = b % 2
                pe.wait_ge(masked, RT * (b + 1))
                for i in range(RT):
                    if i < 2:
                        if b:
                            pe.wait_ge(x2t_done, RT * b)
                    else:
                        pe.wait_ge(at_used, RT * b + i - 1)
                    for j in range(RT):
                        mm = nc.tensor.transpose(b_t[i % 2][:, j * P:(j + 1) * P], adj[:, q, j, i * P:(i + 1) * P],
                                                 ident[:, :])
                    mm.then_inc(at_ps, 1)
                for i in range(RT):
                    pe.wait_ge(x2_ready, RT * b + i + 1)
                    if i < 2:
                        pe.wait_ge(at_used, RT * b + i + 3)
                    else:
                        pe.wait_ge(x2t_done, RT * b + i - 1)
                    for c in range(DC):
                        mm = nc.tensor.transpose(b_t[i % 2][:, c * P:(c + 1) * P], x2[:, i, c * P:(c + 1) * P], ident[:, :])
                    mm.then_inc(x2t_ps, 1)
                if b == 0:
                    pe.wait_ge(rtw_in, 16)
                for i in range(RT):
                    pe.wait_ge(x2t_done, RT * b + i + 1)
                    for c in range(DC):
                        mm = nc.tensor.matmul(ps_logit[:, i * E:(i + 1) * E], x2T[:, i, c], w_rt[:, c, :],
                                              start=(c == 0), stop=(c == DC - 1))
                mm.then_inc(logit_ps, 1)
                if b + 2 < B:
                    stage1(b + 2)
                pe.wait_ge(mask_ready, b + 1)
                if b:
                    pe.wait_ge(msum_ready, b)
                for i in range(RT):
                    dst = ps_rank[:, i * E:(i + 1) * E]
                    nc.tensor.matmul(dst, upper[:, :], mask[:, i], start=True, stop=False)
                    for j in range(i):
                        nc.tensor.matmul(dst, ones[:, :], mask[:, j], start=False, stop=False)
                    mm = nc.tensor.matmul(dst, ones[:, :], msum[:, :], start=False, stop=True)
                mm.then_inc(rank_ps, 1)

                if b == 0:
                    pe.wait_ge(shw_in, 48)

                def up(i):
                    n = RT * b + i
                    if n >= 2:
                        pe.wait_ge(h_ready, n - 1)
                    for c in range(DC):
                        mm = nc.tensor.matmul(b_gu[n % 2][:, :], x2T[:, i, c], w_shgu[:, c, :],
                                              start=(c == 0), stop=(c == DC - 1))
                    mm.then_inc(gu_ps, 1)

                def down(i):
                    n = RT * b + i
                    pe.wait_ge(h_ready, n + 1)
                    if i == 0:
                        pe.wait_ge(s1_done, 7 * min(b + 3, B))
                    if n:
                        pe.wait_ge(ht_done, n)
                    for c in range(IC):
                        mm = nc.tensor.transpose(b_sim[1][:, c * P:(c + 1) * P], h[:, n % 2, c * P:(c + 1) * P], ident[:, :])
                    mm.then_inc(ht_ps, 1)
                    pe.wait_ge(ht_done, n + 1)
                    if n:
                        pe.wait_ge(base_ready, n)
                    for c in range(IC):
                        mm = nc.tensor.matmul(b_y[:, :], hT[:, n % 2, c], w_shdn[:, c, :], start=(c == 0), stop=(c == IC - 1))
                    mm.then_inc(y_ps, 1)

                up(0)
                for i in range(RT):
                    if i + 1 < RT:
                        up(i + 1)
                    down(i)

                pe.wait_ge(slot_oh, b + 1)
                if b:
                    pe.wait_ge(table_used, b)
                for n in range(2 * RT):
                    mm = nc.tensor.matmul(ps_table, oh_slot[:, n], oh_col[:, n].rearrange("p a c -> p (a c)"),
                                          start=(n == 0), stop=(n == 2 * RT - 1))
                mm.then_inc(table_ps, 1)
                if b + 1 < B:
                    check_search(b + 1)

            pe.wait_ge(msum_ready, B)
            nc.tensor.matmul(b_t[0][0:E, 0:1], msum[:, :], ones[:, 0:1], start=True, stop=True).then_inc(fin_t, 1)
            pe.wait_ge(fin_v, 4)
            nc.tensor.matmul(b_t[1][:, 0:1], e_lt[:, :], tiles_e[:, 0:1], start=True, stop=True)
            nc.tensor.matmul(b_t[1][:, 1:2], e_eq[:, :], tiles_e[:, 0:1], start=True, stop=True).then_inc(fin_t, 1)
            pe.wait_ge(fin_v, FIN_V_TABLE)
            nc.tensor.transpose(b_gu[0][:, 0:COLS], table[:, 0], ident[:, :]).then_inc(fin_t, 1)
            pe.wait_ge(fin_v, FIN_V_PLACE)
            nc.tensor.matmul(b_gu[1][:, 0:MT], table_t, place, start=True, stop=True)
            nc.tensor.matmul(b_gu[1][:, 64:64 + MT], e_of[:, :], place, start=True, stop=True).then_inc(fin_t, 1)

            def transpose_in(t, par):
                pe.wait_ge(gathered[par], gather_count(t, par))
                for c in range(DC):
                    mm = nc.tensor.transpose(b_t[par][:, c * P:(c + 1) * P], xg[:, par, c * P:(c + 1) * P], ident[:, :])
                mm.then_inc(m_xt_ps, 1)

            def expert_of(t):
                return pe.value_load(etab[0:1, bass.ds(t, 1)], min_val=0, max_val=E - 1)

            def up_m(t, par):
                e = expert_of(t)
                pe.wait_ge(m_xt, t + 1)
                for c in range(DC):
                    mm = nc.tensor.matmul(b_gu[par][:, :], xgT[:, par, c], w_gu[:, bass.ds(e * (DC * F2) + c * F2, F2)],
                                          start=(c == 0), stop=(c == DC - 1))
                mm.then_inc(m_gu_ps, 1)

            def turn_h(t, par):
                pe.wait_ge(m_h, t + 1)
                for c in range(IC):
                    mm = nc.tensor.transpose(bank[par][:, c * P:(c + 1) * P], h[:, par, c * P:(c + 1) * P], ident[:, :])
                mm.then_inc(m_ht_ps, 1)

            def down_m(t, par):
                e = expert_of(t)
                pe.wait_ge(m_ht, t + 1)
                if not (isinstance(t, int) and t < 2):
                    pe.wait_ge(m_y, t - 1)
                for c in range(IC):
                    mm = nc.tensor.matmul(b_sim[par][:, :], hT[:, par, c], w_dn[:, bass.ds(e * (IC * D) + c * D, D)],
                                          start=(c == 0), stop=(c == IC - 1))
                mm.then_inc(m_y_ps, 1)

            def step(t, par, last=False):
                turn_h(t - 1, 1 - par)
                if not last:
                    transpose_in(t + 1, 1 - par)
                up_m(t, par)
                down_m(t - 1, 1 - par)

            pe.wait_ge(exw_in, 2 * 16 * E)
            pe.wait_ge(fin_v, FIN_V_IDX)
            transpose_in(0, 0)
            transpose_in(1, 1)
            up_m(0, 0)
            step(1, 1)
            step(2, 0)
            with pe.Fori(3, MT - 3, 2) as t:
                step(t, 1)
                step(t + 1, 0)
            step(MT - 2, 1)
            step(MT - 1, 0, True)
            turn_h(MT - 1, 0)
            down_m(MT - 1, 0)

        @block.vector
        def _(dve):
            steps = [0]
            V = nc.vector

            def link(ins):
                steps[0] += 1
                ins.then_inc(vector_step, 1)
                dve.wait_ge(vector_step, steps[0])

            dve.wait_ge(const_ready, 1)

            def fractions():
                link(V.tensor_scalar(part_i[:, 1:2], part_i[:, 0:1], CAP.bit_length() - 1, None, ALU.logical_shift_right))
                link(V.tensor_scalar(part_i[:, 2:3], part_i[:, 0:1], CAP - 1, None, ALU.bitwise_and))
                link(V.tensor_copy(r_of[:, :], part_i[:, 2:3]))
                link(V.tensor_copy(e_of[:, :], part_i[:, 1:2].to_broadcast([P, P])))

            def start_search(b):
                q = b % 2
                dve.wait_ge(x_in[q], 16 * (b // 2 + 1))
                for i in range(RT):
                    ins = V.bn_stats(stats[:, i], xs[:, q, i])
                link(ins)
                for i in range(RT):
                    ins = V.bn_aggr(mv[:, i], stats[:, i])
                link(ins)
                dve.wait_ge(s1_done, 7 * (b + 1))
                link(V.tensor_scalar(mean[:, :], simsum[:, q], 1.0 / N, None, ALU.mult))
                link(V.tensor_tensor(msq[:, :], mean[:, :], mean[:, :], ALU.mult))
                link(V.scalar_tensor_tensor(powin[:, 0], simsq[:, q], 1.0 / N, msq[:, :], ALU.mult, ALU.subtract))
                link(V.tensor_scalar(powin[:, 0], powin[:, 0], 1e-30, None, ALU.max))
                V.tensor_scalar(powin[:, 1], mv[:, :, 1], EPS, None, ALU.add).then_inc(pow_in, 1)
                dve.wait_ge(pow_out, b + 1)
                V.scalar_tensor_tensor(probe[:, 0], powout[:, 0], Z_START, mean[:, :], ALU.mult, ALU.add)
                for n, f in enumerate((1.0, 0.2, 5.0)):
                    V.tensor_scalar(slope[:, n], powout[:, 0], f / DENS, None, ALU.mult)
                link(V.tensor_scalar(xmul[:, :], powout[:, 1], c12[:, 0:1], None, ALU.mult))
                link(V.scalar_tensor_tensor(xadd[:, :], mv[:, :, 0], -1.0, xmul[:, :], ALU.mult, ALU.mult))
                link(V.tensor_scalar(xmul[:, :], xmul[:, :], 1.0, None, ALU.add))
                V.engine_nop().then_inc(affine_in, 1)

            def count(b, k):
                for i in range(RT):
                    ins = V.tensor_scalar(ge[:, i], sim[:, b % 2, i], probe[:, k, i:i + 1], None, ALU.is_ge, ALU.add,
                                          accum_out=cnt[:, k, i:i + 1])
                link(ins)
                V.tensor_scalar(u[:, 0], cnt[:, k], float(KTH), None, ALU.is_ge)
                link(V.tensor_scalar(u[:, 1], cnt[:, k], float(KTH - WIN), None, ALU.is_lt))
                link(V.tensor_tensor(u[:, 0], u[:, 0], u[:, 1], ALU.add))

            def move(k):
                if k:
                    V.tensor_tensor(u[:, 2], cnt[:, k - 1], cnt[:, k], ALU.subtract)
                    link(V.tensor_tensor(u[:, 3], probe[:, k], probe[:, k - 1], ALU.subtract))
                    V.tensor_tensor(u[:, 3], u[:, 3], u[:, 2], ALU.mult)
                    link(V.tensor_tensor(u[:, 2], u[:, 2], u[:, 2], ALU.mult))
                    link(V.tensor_scalar(u[:, 2], u[:, 2], 0.25, None, ALU.max))
                    link(V.reciprocal(u[:, 2], u[:, 2]))
                    link(V.tensor_tensor(u[:, 3], u[:, 3], u[:, 2], ALU.mult))
                    link(V.tensor_tensor(u[:, 3], u[:, 3], slope[:, 1], ALU.max))
                    link(V.tensor_tensor(u[:, 3], u[:, 3], slope[:, 2], ALU.min))
                    by = u[:, 3]
                else:
                    by = slope[:, 0]
                link(V.scalar_tensor_tensor(u[:, 4], cnt[:, k], AIM, by, ALU.subtract, ALU.mult))
                link(V.tensor_tensor(u[:, 4], u[:, 4], u[:, 0], ALU.mult))
                link(V.tensor_tensor(probe[:, k + 1], probe[:, k], u[:, 4], ALU.add))

            def finish_search(b):
                q, k = b % 2, COUNTS - 1
                V.tensor_reduce(u[:, 5, 0:1], u[:, 0], AX_X, ALU.add)
                link(V.tensor_scalar(u[:, 6], cnt[:, k], -1.0, float(KTH - 1), ALU.mult, ALU.add))
                V.tensor_copy(bad[:, :], u[:, 5, 0:1]).then_inc(bad_in, 1)
                for i in range(RT):
                    link(V.scalar_tensor_tensor(tmp[:, i % 2], ge[:, i], -BIG, sim[:, q, i], ALU.mult, ALU.add))
                    ins = V.max(top8[:, i], tmp[:, i % 2])
                link(ins)
                for i in range(RT):
                    ins = V.scalar_tensor_tensor(sel8[:, i], iota8[:, :], u[:, 6, i:i + 1], top8[:, i],
                                                 ALU.is_equal, ALU.mult, accum_out=thr[:, i:i + 1])
                link(ins)
                dve.wait_ge(bad_ps, b + 1)
                link(V.tensor_copy(bad_i[:, :], ps_bad))
                unfinished = dve.value_load(bad_i[0:1, 0:1])
                with dve.If(unfinished > 0):
                    for i in range(RT):
                        V.tensor_copy(tmp[:, 0], sim[:, q, i])
                        dve.drain()
                        with dve.Fori(0, (KTH - 1) // WIN) as _:
                            V.max(top8[:, i], tmp[:, 0])
                            dve.drain()
                            V.match_replace(tmp[:, 0], top8[:, i], tmp[:, 0], -3e38)
                            dve.drain()
                        V.max(top8[:, i], tmp[:, 0])
                        dve.drain()
                        V.tensor_copy(thr[:, i:i + 1], top8[:, i, (KTH - 1) % WIN:(KTH - 1) % WIN + 1])
                        dve.drain()

            def mask_adjacency(b):
                q = b % 2
                for i in range(RT):
                    V.scalar_tensor_tensor(adj[:, q, i], sim[:, q, i], thr[:, i:i + 1], adj[:, q, i],
                                           ALU.is_ge, ALU.mult).then_inc(masked, 1)

            def add_adjacency(b):
                q = b % 2
                dve.wait_ge(affine_out, RT * (b + 1))
                dve.wait_ge(masked, RT * (b + 1))
                for i in range(RT):
                    dve.wait_ge(at_ps, RT * b + i + 1)
                    V.tensor_tensor(tmp[:, i % 2], b_t[i % 2][:, :], adj[:, q, i], ALU.add).then_inc(at_used, 1)
                    dve.wait_ge(at_used, RT * b + i + 1)
                    link(V.scalar_tensor_tensor(xs[:, q, i], tmp[:, i % 2], c12[:, 1:2], xs[:, q, i], ALU.mult, ALU.add))
                    ins = V.bn_stats(stats[:, i], xs[:, q, i])
                link(ins)
                for i in range(RT):
                    ins = V.bn_aggr(mv[:, i], stats[:, i])
                link(ins)
                if b:
                    dve.wait_ge(x2_ready, RT * b)
                V.tensor_scalar(pow2in[:, :], mv[:, :, 1], EPS, None, ALU.add).then_inc(pow2_in, 1)
                dve.wait_ge(pow2_out, b + 1)
                V.scalar_tensor_tensor(x2add[:, :], mv[:, :, 0], -1.0, pow2out[:, :], ALU.mult, ALU.mult).then_inc(x2_in, 1)

            def pick_experts(b):
                dve.wait_ge(logit_ps, b + 1)
                if b:
                    dve.wait_ge(prob_ready, b)
                V.tensor_copy(logit[:, :, :], ps_logit.rearrange("p (i e) -> p i e", e=E)).then_inc(logit_used, 1)
                dve.wait_ge(logit_used, b + 1)
                for i in range(RT):
                    ins = V.max(v8[:, i], logit[:, i])
                link(ins)
                for i in range(RT):
                    ins = V.max_index(i8[:, i], v8[:, i], logit[:, i])
                ins.then_inc(top2, 1)
                dve.wait_ge(top2, b + 1)
                link(V.tensor_copy(ef[:, :, :], i8[:, :, 0:2].rearrange("p i k -> p k i")))
                for k in range(2):
                    ins = V.tensor_tensor(oh[:, k], ef[:, k].unsqueeze(2).to_broadcast([P, RT, E]),
                                          iota8[:, :].unsqueeze(1).to_broadcast([P, RT, E]), ALU.is_equal)
                link(ins)
                V.tensor_tensor(mask[:, :, :], oh[:, 0], oh[:, 1], ALU.add).then_inc(mask_ready, 1)

            def weigh_experts(b):
                dve.wait_ge(prob_ready, b + 1)
                for k in range(2):
                    ins = V.tensor_tensor(ohp[:, k], oh[:, k], prob[:, :, k].unsqueeze(2).to_broadcast([P, RT, E]), ALU.mult)
                link(ins)
                if b:
                    dve.wait_ge(rows_out, 16 * b)
                V.tensor_tensor(x2[:, :, D:ROW], ohp[:, 0], ohp[:, 1], ALU.add).then_inc(payload, 1)

            def rank_tokens(b):
                dve.wait_ge(rank_ps, b + 1)
                for k in range(2):
                    ins = V.tensor_tensor(rsel[:, k].rearrange("p i e -> p (i e)"), oh[:, k].rearrange("p i e -> p (i e)"),
                                          ps_rank, ALU.mult)
                link(ins)
                link(V.tensor_reduce(rank[:, :], rsel[:, :, :, :].rearrange("p k i e -> p (k i) e"), AX_X, ALU.add))
                link(V.tensor_reduce(mred[:, :], mask[:, :, :].rearrange("p i e -> p e i"), AX_X, ALU.add))
                V.tensor_tensor(msum[:, :], msum[:, :], mred[:, :], ALU.add).then_inc(msum_ready, 1)
                link(V.tensor_copy(rank_i[:, 0], rank[:, :]))
                V.tensor_scalar(rank_i[:, 1], rank_i[:, 0], P.bit_length() - 1, None, ALU.logical_shift_right)
                link(V.tensor_scalar(rank_i[:, 2], rank_i[:, 0], P - 1, None, ALU.bitwise_and))
                link(V.tensor_copy(rank_f[:, :, :], rank_i[:, 1:3]))
                V.scalar_tensor_tensor(col[:, :], ef[:, :, :].rearrange("p k i -> p (k i)"), float(CAP), rank_f[:, 0],
                                       ALU.mult, ALU.add)
                link(V.scalar_tensor_tensor(delta[:, :], rank_f[:, 1], -1.0, part[:, 0:1].to_broadcast([P, 2 * RT]),
                                            ALU.mult, ALU.add))
                if b:
                    dve.wait_ge(table_ps, b)
                for n in range(2 * RT):
                    tile = float(RT * b + n % RT - CAP)
                    V.tensor_scalar(oh_slot[:, n], iota_b[:, :], rank_f[:, 1, n:n + 1], None, ALU.is_equal)
                    V.tensor_scalar(oh_col[:, n, 0], iota_b[:, :], col[:, n:n + 1], tile, ALU.is_equal, ALU.mult)
                    ins = V.tensor_scalar(oh_col[:, n, 1], iota_b[:, :], col[:, n:n + 1], delta[:, n:n + 1],
                                          ALU.is_equal, ALU.mult)
                ins.then_inc(slot_oh, 1)

            def gate_hidden(b, i):
                n = RT * b + i
                dve.wait_ge(silu_ready, n + 1)
                if n >= 2:
                    dve.wait_ge(ht_ps, n - 1)
                V.tensor_tensor(h[:, n % 2], b_gu[n % 2][:, I:F2], silu[:, n % 2], ALU.mult).then_inc(h_ready, 1)

            def make_base(b, i):
                n = RT * b + i
                dve.wait_ge(y_ps, n + 1)
                V.scalar_tensor_tensor(xs[:, b % 2, i], b_y[:, :], gates[:, 1:2], xs[:, b % 2, i],
                                       ALU.mult, ALU.add).then_inc(base_ready, 1)

            def keep_table(b):
                dve.wait_ge(table_ps, b + 1)
                dst = table[:, :, :].rearrange("p a c -> p (a c)")
                if b == 0:
                    V.tensor_copy(dst, ps_table).then_inc(table_used, 1)
                else:
                    V.tensor_tensor(dst, dst, ps_table, ALU.add).then_inc(table_used, 1)
                dve.wait_ge(table_used, b + 1)

            fractions()
            dve.wait_ge(gates_ready, 1)
            link(V.tensor_tensor(c12[:, 2:3], gates[:, 2:3], gates[:, 0:1], ALU.mult))
            link(V.tensor_tensor(c12[:, 0:1], gates[:, 0:1], c12[:, 2:3], ALU.subtract))
            link(V.tensor_scalar(c12[:, 1:2], c12[:, 2:3], 0.5, None, ALU.mult))
            start_search(0)
            for k in range(COUNTS):
                count(0, k)
                if k + 1 < COUNTS:
                    move(k)
            finish_search(0)
            mask_adjacency(0)
            add_adjacency(0)
            for b in range(B):
                more = b + 1 < B
                if more:
                    start_search(b + 1)
                    count(b + 1, 0)
                    move(0)
                pick_experts(b)
                weigh_experts(b)
                if more:
                    count(b + 1, 1)
                    move(1)
                rank_tokens(b)
                gate_hidden(b, 0)
                gate_hidden(b, 1)
                for k in range(2, COUNTS):
                    if more:
                        count(b + 1, k)
                        if k + 1 < COUNTS:
                            move(k)
                    make_base(b, k - 2)
                    if k < RT:
                        gate_hidden(b, k)
                make_base(b, 3)
                keep_table(b)
                if more:
                    finish_search(b + 1)
                    mask_adjacency(b + 1)
                    add_adjacency(b + 1)

            done = [0]

            def fin(ins):
                done[0] += 1
                ins.then_inc(fin_v, 1)
                dve.wait_ge(fin_v, done[0])

            dve.wait_ge(fin_t, 1)
            fin(V.tensor_copy(n_e[:, 0:1], b_t[0][0:E, 0:1]))
            fin(V.tensor_scalar(tiles_e[:, 1:2], b_t[0][0:E, 0:1], float(P - 1), None, ALU.add))
            fin(V.tensor_copy(n_e[:, 0:1], tiles_e[:, 1:2]))
            link(V.tensor_scalar(n_e[:, 1:2], n_e[:, 0:1], P.bit_length() - 1, None, ALU.logical_shift_right))
            fin(V.tensor_copy(tiles_e[:, 0:1], n_e[:, 1:2]))
            fin(V.scalar_tensor_tensor(table[:, 0], table[:, 0], float(P), table[:, 1], ALU.mult, ALU.add))
            assert done[0] == FIN_V_TABLE
            dve.wait_ge(fin_t, 2)
            link(V.tensor_copy(tile_pos[:, 0:2], b_t[1][:, 0:2]))
            link(V.tensor_tensor(tile_pos[:, 1:2], tile_pos[:, 1:2], r_of[:, :], ALU.is_gt))
            link(V.tensor_tensor(tile_pos[:, 0:1], tile_pos[:, 0:1], r_of[:, :], ALU.add))
            link(V.scalar_tensor_tensor(tile_pos[:, 2:3], tile_pos[:, 0:1], 1.0, tile_pos[:, 1:2], ALU.add, ALU.mult))
            link(V.tensor_scalar(tile_pos[:, 3:4], tile_pos[:, 2:3], 1.0, None, ALU.subtract))
            link(V.tensor_scalar(place, iota_m[:, :], tile_pos[:, 3:4], None, ALU.is_equal))
            dve.wait_ge(fin_t, 3)
            fin(V.tensor_copy(table_t, b_gu[0][:, 0:COLS]))
            assert done[0] == FIN_V_PLACE
            dve.wait_ge(fin_t, 4)
            V.tensor_scalar(idx[:, :], b_gu[1][:, 0:MT], part[:, 0:1], float(T), ALU.add, ALU.add)
            V.tensor_copy(etab[:, :], b_gu[1][0:1, 64:64 + MT])
            fin(V.tensor_tensor(oh_e, b_gu[1][:, 64:64 + MT].unsqueeze(2).to_broadcast([P, MT, E]),
                                iota8[:, :].unsqueeze(1).to_broadcast([P, MT, E]), ALU.is_equal))
            assert done[0] == FIN_V_IDX

            def weight_of(t, par):
                dve.wait_ge(gathered[par], gather_count(t, par))
                V.scalar_tensor_tensor(p_junk[:, par], xg[:, par, D:ROW], 1.0, adj[:, 0, 1, bass.ds(t * E, E)],
                                       ALU.mult, ALU.mult, accum_out=p_t[:, par:par + 1]).then_inc(m_p, 1)

            def gate(t, par):
                dve.wait_ge(m_silu, t + 1)
                dve.wait_ge(m_p, t + 1)
                V.scalar_tensor_tensor(h[:, par], b_gu[par][:, I:F2], p_t[:, par:par + 1], silu[:, par],
                                       ALU.mult, ALU.mult).then_inc(m_h, 1)

            def ht_out(t, par):
                dve.wait_ge(m_ht_ps, t + 1)
                V.tensor_copy(hT[:, par], bank[par][:, 0:I].rearrange("p (c t) -> p c t", c=IC)).then_inc(m_ht, 1)

            def step(t, par, last=False):
                if not (isinstance(t, int) and t < 3):
                    dve.wait_ge(m_y_ps, t - 2)
                ht_out(t - 1, 1 - par)
                if not last:
                    weight_of(t + 1, 1 - par)
                gate(t, par)

            weight_of(0, 0)
            weight_of(1, 1)
            gate(0, 0)
            step(1, 1)
            step(2, 0)
            with dve.Fori(3, MT - 3, 2) as t:
                step(t, 1)
                step(t + 1, 0)
            step(MT - 2, 1)
            step(MT - 1, 0, True)
            dve.wait_ge(m_y_ps, MT - 2)
            ht_out(MT - 1, 0)


FIN_V_TABLE, FIN_V_PLACE, FIN_V_IDX = 5, 6, 7


def gather_count(t, par):
    return 8 * t + (8 if par else 16)


_INS = ["x", "ctx_512", "g_xattn", "g_ffn", "L0_xattn_Wq", "L0_xattn_Wk", "L0_xattn_gamma_raw", "L0_ffn_router_w",
        "L0_ffn_gate_up_w", "L0_ffn_down_w", "L0_ffn_shared_gate_w", "L0_ffn_shared_up_w", "L0_ffn_shared_down_w"]


def kernel(**inputs):
    import numpy as _np
    import concourse.bacc as _bacc
    from concourse import mybir as _mybir
    from concourse.bass_utils import run_bass_kernel_spmd as _run

    nc = _bacc.Bacc("TRN2", target_bir_lowering=False, num_devices=1)
    arrays, args = {}, []
    for name in _INS:
        a = _np.ascontiguousarray(inputs[name])
        if a.size == 1:
            a = a.reshape(1, 1)
        arrays[f"in_{name}_dram"] = a
        args.append(nc.dram_tensor(f"in_{name}_dram", a.shape, _mybir.dt.from_np(a.dtype), kind="ExternalInput").ap())
    b, n, d = inputs["x"].shape
    out = nc.dram_tensor("out_dram", (b * n + 128, d), _mybir.dt.from_np(_np.dtype("float32")), kind="ExternalOutput").ap()
    flamingo_gated_block(nc, *args, out)
    r = _run(nc, [arrays], core_ids=[0])
    return r.results[0]["out_dram"][:b * n].reshape(b, n, d)
```

```python
from contextlib import ExitStack

import concourse.bass as bass
from concourse import mybir

F32 = mybir.dt.float32
BF16 = mybir.dt.bfloat16
I32 = mybir.dt.int32
U32 = mybir.dt.uint32
U8 = mybir.dt.uint8
I8 = mybir.dt.int8
ALU = mybir.AluOpType
ACT = mybir.ActivationFunctionType
AX_X = mybir.AxisListType.X

P = 128
EPS = 1e-5
TOP_K_RATIO = 0.3
HEADS = 4
BIG = 1e30
COUNTS = 5
Z_START = 0.52


def flamingo_gated_block(nc, x, ctx_in, g_xattn, g_ffn, wq, wk, gamma_raw, router_w, gate_up_w, down_w,
                         sh_gate_w, sh_up_w, sh_down_w, out):
    B, N, D = x.shape
    C = ctx_in.shape[2]
    E, _, F2 = gate_up_w.shape
    I = F2 // 2
    T = B * N
    RT = N // P
    DC = D // P
    IC = I // P
    CAP = T // P
    COLS = E * CAP
    MT = 2 * T // P + E - 1
    ROW = D + E
    SCALE = 1.0 / (float(C // HEADS) ** 0.5 * HEADS)
    KTH = max(1, int(N * TOP_K_RATIO))
    WIN = 8
    AIM = KTH - WIN / 2 - 0.5
    DONE = (WIN / 2) ** 2 - 1.0
    SHARE = RT // 2
    DENS = N * 0.348
    assert C == P and N == D == 512 and COLS == P and F2 == 512 and RT == 4

    x2_rows = nc.dram_tensor("x2_rows", (T + P, ROW), F32).ap()

    with ExitStack() as stack:
        def sb(name, shape, dt=F32):
            return stack.enter_context(nc.sbuf_tensor(name, shape, dt))

        def sem(name):
            return stack.enter_context(nc.semaphore(name))

        w_gu = sb("w_gu", [P, E * DC * F2])
        w_dn = sb("w_dn", [P, E * IC * D])
        w_shgu = sb("w_shgu", [P, DC, F2])
        w_shdn = sb("w_shdn", [P, IC, D])
        w_rt = sb("w_rt", [P, DC, E])
        wqkT = sb("wqkT", [P, 2, C])
        ctx_sb = sb("ctx_sb", [P, RT, C])
        ctxT = sb("ctxT", [P, N])
        qT = sb("qT", [P, N])
        kT = sb("kT", [P, N])
        sim = sb("sim", [P, 2, RT, N])
        adj = sb("adj", [P, 2, RT, N])
        ge = sb("ge", [P, RT, N], U8)
        tmp = sb("tmp", [P, 2, N])
        xs = sb("xs", [P, 2, RT, D])
        x2 = sb("x2", [P, RT, ROW])
        x2T = sb("x2T", [P, RT, DC, P])
        silu = sb("silu", [P, 2, I])
        h = sb("h", [P, 2, I])
        hT = sb("hT", [P, 2, IC, P])
        scal = sb("scal", [1, 4])
        scal_t = sb("scal_t", [1, 4])
        gates = sb("gates", [P, 4])
        c12 = sb("c12", [P, 4])
        simsum = sb("simsum", [P, 2, RT])
        simsq = sb("simsq", [P, 2, RT])
        mean = sb("mean", [P, RT])
        msq = sb("msq", [P, RT])
        powin = sb("powin", [P, 2, RT])
        powexp = sb("powexp", [P, 2, RT])
        powout = sb("powout", [P, 2, RT])
        pow2in = sb("pow2in", [P, RT])
        pow2out = sb("pow2out", [P, RT])
        stats = sb("stats", [P, RT, 6])
        mv = sb("mv", [P, RT, 2])
        xmul = sb("xmul", [P, RT])
        xadd = sb("xadd", [P, RT])
        x2add = sb("x2add", [P, RT])
        dev = sb("dev", [P, RT])
        probe = sb("probe", [P, COUNTS, RT])
        cnt = sb("cnt", [P, COUNTS, RT])
        sgn = sb("sgn", [P, COUNTS, RT])
        err = sb("err", [P, COUNTS, RT])
        dz = sb("dz", [P, COUNTS, RT])
        u = sb("u", [P, 8, RT])
        top8 = sb("top8", [P, RT, 8])
        sel8 = sb("sel8", [P, RT, 8])
        thr = sb("thr", [P, RT])
        bad = sb("bad", [P, RT], BF16)
        bad_f = sb("bad_f", [1, 1])
        bad_i = sb("bad_i", [1, RT + 1], I32)
        logit = sb("logit", [P, RT, E])
        v8 = sb("v8", [P, RT, 8])
        i8 = sb("i8", [P, RT, 8], U32)
        prob = sb("prob", [P, RT, 2])
        ef = sb("ef", [P, 2, RT])
        oh = sb("oh", [P, 2, RT, E])
        ohp = sb("ohp", [P, 2, RT, E])
        mask = sb("mask", [P, RT, E], BF16)
        msum = sb("msum", [P, E], BF16)
        mred = sb("mred", [P, E])
        rsel = sb("rsel", [P, 2, RT, E])
        rank = sb("rank", [P, 2 * RT])
        rank_i = sb("rank_i", [P, 3, 2 * RT], I32)
        rank_f = sb("rank_f", [P, 2, 2 * RT])
        col = sb("col", [P, 2 * RT])
        delta = sb("delta", [P, 2 * RT])
        oh_slot = sb("oh_slot", [P, 2 * RT, P], BF16)
        oh_col = sb("oh_col", [P, 2 * RT, 2, COLS], BF16)
        table = sb("table", [P, 2, COLS])
        n_e = sb("n_e", [E, 2], I32)
        tiles_e = sb("tiles_e", [E, 2])
        tiles_b = sb("tiles_b", [E, 1], BF16)
        tile_pos = sb("tile_pos", [P, 4])
        idx = sb("idx", [P, MT], I32)
        etab = sb("etab", [1, MT], I32)
        p_t = sb("p_t", [P, 2])
        p_junk = sb("p_junk", [P, 2, E])
        ident = sb("ident", [P, P])
        upper = sb("upper", [P, P], BF16)
        ones = sb("ones", [P, P], BF16)
        ones_f = sb("ones_f", [P, P])
        iota_b = sb("iota_b", [P, P], BF16)
        iota8 = sb("iota8", [P, 8])
        iota_m = sb("iota_m", [P, MT])
        part = sb("part", [P, 1])
        e_of = sb("e_of", [P, P])
        r_of = sb("r_of", [P, 1])
        e_lt = sb("e_lt", [E, COLS], BF16)
        e_eq = sb("e_eq", [E, COLS], BF16)
        part_i = sb("part_i", [P, 3], I32)

        bank = [stack.enter_context(nc.psum_tensor(f"bank{n}", [P, 512], F32)) for n in range(8)]
        b_small, b_sim, b_t, b_gu = bank[0], bank[2:4], bank[4:6], bank[6:8]
        b_y = [bank[1], bank[2]]
        ps_logit = b_small[:, 0:RT * E]
        ps_rank = b_small[:, 32:32 + RT * E]
        ps_bad = b_t[0][0:1, 0:RT]
        ps_table = b_small[:, 256:512]
        xg, xgT, y_sb = x2, x2T, tmp
        wqk = tmp[:, :, 0:C]
        late = adj[:, 0, :, :].rearrange("p i n -> p (i n)")
        table_t = late[:, 0:COLS]
        place = late[:, COLS:COLS + MT]
        oh_e = late[:, 512:512 + MT * E].rearrange("p (t e) -> p t e", e=E)
        zeros = x2[:, 0]

        ctx_loaded = sem("ctx_loaded")
        x_in = [sem("x_in_even"), sem("x_in_odd")]
        wqk_in = sem("wqk_in")
        scal_in = sem("scal_in")
        shw_in = sem("shw_in")
        rtw_in = sem("rtw_in")
        exw_in = sem("exw_in")
        pool_step = sem("pool_step")
        const_ready = sem("const_ready")
        zero_ready = sem("zero_ready")
        scal_ready = sem("scal_ready")
        gates_bc = sem("gates_bc")
        gates_ready = sem("gates_ready")
        wT_ps = sem("wT_ps")
        wT_ready = sem("wT_ready")
        s1_ps = sem("s1_ps")
        s1_done = sem("s1_done")
        pow_in = sem("pow_in")
        pow_out = sem("pow_out")
        affine_in = sem("affine_in")
        affine_out = sem("affine_out")
        probe_ready = sem("probe_ready")
        sign_ready = sem("sign_ready")
        below_ready = sem("below_ready")
        top8_ready = sem("top8_ready")
        bad_in = sem("bad_in")
        bad_ps = sem("bad_ps")
        masked = sem("masked")
        at_ps = sem("at_ps")
        at_used = sem("at_used")
        pow2_in = sem("pow2_in")
        pow2_out = sem("pow2_out")
        x2_in = sem("x2_in")
        x2_ready = sem("x2_ready")
        x2t_ps = sem("x2t_ps")
        x2t_done = sem("x2t_done")
        logit_ps = sem("logit_ps")
        logit_used = sem("logit_used")
        top2 = sem("top2")
        prob_ready = sem("prob_ready")
        mask_ready = sem("mask_ready")
        msum_ready = sem("msum_ready")
        rank_ps = sem("rank_ps")
        payload = sem("payload")
        slot_known = sem("slot_known")
        slot_oh = sem("slot_oh")
        table_ps = sem("table_ps")
        table_used = sem("table_used")
        fin_v = sem("fin_v")
        fin_t = sem("fin_t")
        gu_ps = sem("gu_ps")
        silu_ready = sem("silu_ready")
        h_ready = sem("h_ready")
        ht_ps = sem("ht_ps")
        ht_done = sem("ht_done")
        y_ps = sem("y_ps")
        base_ready = sem("base_ready")
        rows_out = sem("rows_out")
        base_out = sem("base_out")
        dummy_out = sem("dummy_out")
        gathered = [sem("gathered_even"), sem("gathered_odd")]
        scattered = sem("scattered")
        m_xt_ps = sem("m_xt_ps")
        m_xt = sem("m_xt")
        m_gu_ps = sem("m_gu_ps")
        m_p = sem("m_p")
        m_silu = sem("m_silu")
        m_h = sem("m_h")
        m_ht_ps = sem("m_ht_ps")
        m_ht = sem("m_ht")
        m_y_ps = sem("m_y_ps")
        m_y = sem("m_y")
        vector_step = sem("vector_step")
        scalar_step = sem("scalar_step")

        x_v = x.rearrange("b (i p) d -> b p i d", p=P)
        ctx_v = ctx_in.rearrange("b (i p) d -> b p i d", p=P)
        out_v = out[0:T, :].rearrange("(b i p) d -> b p i d", p=P, i=RT)
        rows_v = x2_rows[0:T, :].rearrange("(b i p) d -> b p i d", p=P, i=RT)

        block = stack.enter_context(nc.Block())

        @block.sync
        def _(sp):
            def load_ctx(b):
                sp.wait_ge(s1_ps, 7 * (b - 1) + 1)
                sp.dma_start(ctx_sb[:, :, :], ctx_v[b]).then_inc(ctx_loaded, 16)

            def load_x(b):
                if b >= 2:
                    sp.wait_ge(base_out, 16 * (b - 1))
                sp.dma_start(xs[:, b % 2], x_v[b]).then_inc(x_in[b % 2], 16)

            sp.dma_start(ctx_sb[:, :, :], ctx_v[0]).then_inc(ctx_loaded, 16)
            sp.dma_start(wqk[:, 0], wq).then_inc(wqk_in, 16)
            sp.dma_start(wqk[:, 1], wk).then_inc(wqk_in, 16)
            for n, g in enumerate((g_xattn, g_ffn, gamma_raw)):
                sp.dma_start(scal[0:1, n:n + 1], g).then_inc(scal_in, 16)
            load_x(0)
            load_ctx(1)
            load_x(1)
            sp.dma_start(w_rt[:, :, :], router_w.rearrange("(c p) e -> p c e", p=P)).then_inc(rtw_in, 16)
            sp.dma_start(w_shgu[:, :, 0:I], sh_gate_w.rearrange("(c p) f -> p c f", p=P)).then_inc(shw_in, 16)
            sp.dma_start(w_shgu[:, :, I:F2], sh_up_w.rearrange("(c p) f -> p c f", p=P)).then_inc(shw_in, 16)
            sp.dma_start(w_shdn[:, :, :], sh_down_w.rearrange("(c p) d -> p c d", p=P)).then_inc(shw_in, 16)
            sp.wait_ge(zero_ready, 1)
            sp.dma_start(x2_rows[T:T + P, :], zeros).then_inc(dummy_out, 16)
            sp.dma_start(out[T:T + P, :], x2[:, 0, 0:D]).then_inc(dummy_out, 16)
            for e in range(E):
                sp.dma_start(w_gu[:, e * DC * F2:(e + 1) * DC * F2].rearrange("p (c f) -> p c f", c=DC),
                             gate_up_w[e].rearrange("(c p) f -> p c f", p=P)).then_inc(exw_in, 16)
                sp.dma_start(w_dn[:, e * IC * D:(e + 1) * IC * D].rearrange("p (c d) -> p c d", c=IC),
                             down_w[e].rearrange("(c p) d -> p c d", p=P)).then_inc(exw_in, 16)
            for b in range(B):
                if b + 2 < B:
                    load_ctx(b + 2)
                sp.wait_ge(x2_ready, RT * (b + 1))
                sp.wait_ge(payload, b + 1)
                sp.dma_start(rows_v[b], x2[:, :, :]).then_inc(rows_out, 16)
                sp.wait_ge(base_ready, RT * (b + 1))
                sp.dma_start(out_v[b], xs[:, b % 2]).then_inc(base_out, 16)
                if b + 2 < B:
                    load_x(b + 2)
            sp.wait_ge(rows_out, 16 * B)
            sp.wait_ge(base_out, 16 * B)
            sp.wait_ge(dummy_out, 32)
            sp.wait_ge(scattered, 16 * MT)

        @block.gpsimd
        def _(pool):
            steps = [0]

            def link(ins):
                steps[0] += 1
                ins.then_inc(pool_step, 1)
                pool.wait_ge(pool_step, steps[0])

            nc.gpsimd.memset(zeros, 0.0).then_inc(zero_ready, 1)
            nc.gpsimd.memset(ones[:, :], 1.0)
            nc.gpsimd.memset(ones_f[:, :], 1.0)
            nc.gpsimd.memset(e_lt[:, :], 1.0)
            nc.gpsimd.memset(e_eq[:, :], 1.0)
            nc.gpsimd.memset(msum[:, :], 0.0)
            nc.gpsimd.memset(powexp[:, 0], 0.5)
            link(nc.gpsimd.memset(powexp[:, 1], -0.5))
            nc.gpsimd.affine_select(out=ident[:, :], in_=ones_f[:, :], compare_op=ALU.is_equal, fill=0.0, base=0,
                                    pattern=[[-1, P]], channel_multiplier=1)
            nc.gpsimd.affine_select(out=upper[:, :], in_=ones[:, :], compare_op=ALU.is_gt, fill=0.0, base=0,
                                    pattern=[[1, P]], channel_multiplier=-1)
            nc.gpsimd.affine_select(out=e_lt[:, :], in_=e_lt[:, :], compare_op=ALU.is_ge, fill=0.0, base=-CAP,
                                    pattern=[[1, COLS]], channel_multiplier=-CAP)
            link(nc.gpsimd.affine_select(out=e_eq[:, :], in_=e_eq[:, :], compare_op=ALU.is_ge, fill=0.0, base=0,
                                         pattern=[[1, COLS]], channel_multiplier=-CAP))
            nc.gpsimd.affine_select(out=e_eq[:, :], in_=e_eq[:, :], compare_op=ALU.is_ge, fill=0.0, base=CAP - 1,
                                    pattern=[[-1, COLS]], channel_multiplier=CAP)
            nc.gpsimd.iota(iota_b[:, :], [[1, P]], base=0, channel_multiplier=0, allow_small_or_imprecise_dtypes=True)
            nc.gpsimd.iota(iota8[:, :], [[1, 8]], base=0, channel_multiplier=0, allow_small_or_imprecise_dtypes=True)
            nc.gpsimd.iota(iota_m[:, :], [[1, MT]], base=0, channel_multiplier=0, allow_small_or_imprecise_dtypes=True)
            nc.gpsimd.iota(part[:, :], [[0, 1]], base=0, channel_multiplier=1, allow_small_or_imprecise_dtypes=True)
            nc.gpsimd.iota(part_i[:, 0:1], [[0, 1]], base=0, channel_multiplier=1).then_inc(const_ready, 1)

            def one_hots(b):
                pool.wait_ge(slot_known, b + 1)
                if b:
                    pool.wait_ge(table_ps, b)
                for n in range(2 * RT):
                    tile = float(RT * b + n % RT - CAP)
                    nc.gpsimd.tensor_scalar(oh_slot[:, n], iota_b[:, :], rank_f[:, 1, n:n + 1], None, ALU.is_equal)
                    nc.gpsimd.tensor_scalar(oh_col[:, n, 0], iota_b[:, :], col[:, n:n + 1], tile, ALU.is_equal, ALU.mult)
                    ins = nc.gpsimd.tensor_scalar(oh_col[:, n, 1], iota_b[:, :], col[:, n:n + 1], delta[:, n:n + 1],
                                                  ALU.is_equal, ALU.mult)
                ins.then_inc(slot_oh, 1)

            for b in range(B):
                pool.wait_ge(pow_in, b + 1)
                nc.gpsimd.tensor_tensor(powout[:, :, :], powin[:, :, :], powexp[:, :, :], ALU.pow).then_inc(pow_out, 1)
                pool.wait_ge(affine_in, b + 1)
                for i in range(RT):
                    nc.gpsimd.tensor_scalar(xs[:, b % 2, i], xs[:, b % 2, i], xmul[:, i:i + 1], xadd[:, i:i + 1],
                                            ALU.mult, ALU.add).then_inc(affine_out, 1)
                if b:
                    one_hots(b - 1)
                pool.wait_ge(pow2_in, b + 1)
                nc.gpsimd.tensor_tensor(pow2out[:, :], pow2in[:, :], powexp[:, 1], ALU.pow).then_inc(pow2_out, 1)

            pool.wait_ge(fin_v, FIN_V_IDX)
            pool.wait_ge(dummy_out, 32)

            def gather(t):
                nc.gpsimd.indirect_dma_start(out=xg[:, t % 2, :], out_offset=None, in_=x2_rows[:, :],
                                             in_offset=bass.IndirectOffsetOnAxis(ap=idx[:, t:t + 1], axis=0)
                                             ).then_inc(gathered[t % 2], 16)

            def scatter(t):
                nc.gpsimd.indirect_dma_start(out=out[:, :],
                                             out_offset=bass.IndirectOffsetOnAxis(ap=idx[:, t:t + 1], axis=0),
                                             in_=y_sb[:, t % 2, :], in_offset=None, compute_op=ALU.add
                                             ).then_inc(scattered, 16)

            pool.wait_ge(rows_out, 16 * B)
            gather(0)
            gather(1)
            pool.wait_ge(base_out, 16 * B)
            for t in range(MT):
                if t + 2 < MT:
                    pool.wait_ge(m_xt_ps, t + 1)
                    pool.wait_ge(m_p, t + 1)
                    gather(t + 2)
                if t:
                    if t >= 2:
                        pool.wait_ge(scattered, 16 * (t - 1))
                    pool.wait_ge(m_y, t)
                    scatter(t - 1)
            pool.wait_ge(scattered, 16 * (MT - 1))
            pool.wait_ge(m_y, MT)
            scatter(MT - 1)

        @block.scalar
        def _(act):
            act.wait_ge(scal_in, 48)
            nc.scalar.activation(scal_t[0:1, 0:2], scal[0:1, 0:2], ACT.Tanh)
            nc.scalar.activation(scal_t[0:1, 2:3], scal[0:1, 2:3], ACT.Sigmoid).then_inc(scal_ready, 1)
            act.wait_ge(gates_bc, 1)
            nc.scalar.copy(gates[:, 0:3], b_small[:, 0:3]).then_inc(gates_ready, 1)
            act.wait_ge(wT_ps, 1)
            nc.scalar.copy(wqkT[:, :, :], b_t[0][:, 0:2 * C].rearrange("p (a c) -> p a c", a=2)).then_inc(wT_ready, 1)

            def stage1_in(b):
                for j, dst in enumerate((ctxT, qT, kT)):
                    act.wait_ge(s1_ps, 7 * b + j + 1)
                    nc.scalar.copy(dst[:, :], b_sim[j % 2][:, :]).then_inc(s1_done, 1)

            def stage1_out(b, tiles=range(RT)):
                q = b % 2
                for i in tiles:
                    ps = b_sim[(3 + i) % 2]
                    act.wait_ge(s1_ps, 7 * b + i + 4)
                    if b >= 2 and i == 0:
                        act.wait_ge(masked, RT * (b - 1))
                        act.wait_ge(at_ps, RT * (b - 1))
                    nc.scalar.activation(sim[:, q, i], ps[:, :], ACT.Copy, accum_out=simsum[:, q, i:i + 1])
                    nc.scalar.activation(adj[:, q, i], ps[:, :], ACT.Square,
                                         accum_out=simsq[:, q, i:i + 1]).then_inc(scalar_step, 1)
                    act.wait_ge(scalar_step, RT * b + i + 1)
                    nc.scalar.activation(adj[:, q, i], ps[:, :], ACT.Sigmoid, scale=SCALE).then_inc(s1_done, 1)

            def count(b, k):
                act.wait_ge(probe_ready, (COUNTS - 1) * b + k + 1)
                for i in range(SHARE, RT):
                    ins = nc.scalar.activation(ge[:, i].bitcast(I8), sim[:, b % 2, i], ACT.Sign, scale=-1.0,
                                               bias=probe[:, k, i:i + 1], accum_out=sgn[:, k, i:i + 1])
                ins.then_inc(sign_ready, 1)

            stage1_in(0)
            stage1_out(0)
            for k in range(COUNTS - 1):
                count(0, k)
                if k == 0:
                    stage1_in(1)
                if k == 1:
                    stage1_out(1)
            for b in range(B):
                more = b + 1 < B
                if b + 2 < B:
                    stage1_in(b + 2)
                act.wait_ge(x2_in, b + 1)
                if b:
                    act.wait_ge(rows_out, 16 * b)
                else:
                    act.wait_ge(dummy_out, 32)
                for i in range(RT):
                    nc.scalar.activation(x2[:, i, 0:D], xs[:, b % 2, i], ACT.Identity, scale=pow2out[:, i:i + 1],
                                         bias=x2add[:, i:i + 1]).then_inc(x2_ready, 1)
                if more:
                    count(b + 1, 0)
                for i in range(RT):
                    act.wait_ge(x2t_ps, RT * b + i + 1)
                    if b and i == 0:
                        act.wait_ge(gu_ps, RT * b)
                    nc.scalar.copy(x2T[:, i], b_t[i % 2][:, :].rearrange("p (c t) -> p c t", c=DC)).then_inc(x2t_done, 1)

                def silu_of(i):
                    n = RT * b + i
                    act.wait_ge(gu_ps, n + 1)
                    if n >= 2:
                        act.wait_ge(h_ready, n - 1)
                    nc.scalar.activation(silu[:, n % 2], b_gu[n % 2][:, 0:I], ACT.Silu).then_inc(silu_ready, 1)

                def ht_of(i):
                    n = RT * b + i
                    act.wait_ge(ht_ps, n + 1)
                    if n >= 2:
                        act.wait_ge(y_ps, n - 1)
                    nc.scalar.copy(hT[:, n % 2], b_sim[1][:, 0:I].rearrange("p (c t) -> p c t", c=IC)).then_inc(ht_done, 1)

                for k in (1, 2):
                    if more:
                        count(b + 1, k)
                    if b + 2 < B:
                        stage1_out(b + 2, (2 * k - 2, 2 * k - 1))
                    if k == 2:
                        act.wait_ge(top2, b + 1)
                        if b:
                            act.wait_ge(payload, b)
                        nc.scalar.activation(prob[:, :, :], v8[:, :, 0:2], ACT.Sigmoid).then_inc(prob_ready, 1)
                if more:
                    count(b + 1, 3)
                silu_of(0)
                silu_of(1)
                for i in range(RT):
                    ht_of(i)
                    if i + 2 < RT:
                        silu_of(i + 2)

            def xt_out(t, par):
                act.wait_ge(m_xt_ps, t + 1)
                nc.scalar.copy(xgT[:, par], b_t[par][:, :].rearrange("p (c t) -> p c t", c=DC)).then_inc(m_xt, 1)

            def silu_out(t, par):
                act.wait_ge(m_gu_ps, t + 1)
                act.wait_ge(m_p, t + 1)
                nc.scalar.activation(silu[:, par], b_gu[par][:, 0:I], ACT.Silu, scale=p_t[:, par:par + 1]).then_inc(m_silu, 1)

            def y_out(t, par):
                act.wait_ge(m_y_ps, t + 1)
                nc.scalar.activation(y_sb[:, par], b_sim[par][:, :], ACT.Copy, scale=gates[:, 1:2]).then_inc(m_y, 1)

            act.wait_ge(gu_ps, T // P)
            xt_out(0, 0)
            xt_out(1, 1)
            act.wait_ge(h_ready, T // P)
            silu_out(0, 0)

            def step(t, par, last=False):
                if not last:
                    act.wait_ge(m_gu_ps, t)
                    xt_out(t + 1, 1 - par)
                silu_out(t, par)
                if not (isinstance(t, int) and t < 3):
                    act.wait_ge(scattered, 16 * (t - 2))
                y_out(t - 1, 1 - par)

            step(1, 1)
            step(2, 0)
            with act.Fori(3, MT - 3, 2) as t:
                step(t, 1)
                step(t + 1, 0)
            step(MT - 2, 1)
            step(MT - 1, 0, True)
            act.wait_ge(scattered, 16 * (MT - 2))
            y_out(MT - 1, 0)

        @block.tensor
        def _(pe):
            pe.wait_ge(const_ready, 1)
            pe.wait_ge(wqk_in, 32)
            nc.tensor.transpose(b_t[0][:, 0:C], wqk[:, 0], ident[:, :])
            nc.tensor.transpose(b_t[0][:, C:2 * C], wqk[:, 1], ident[:, :]).then_inc(wT_ps, 1)

            def stage1_in(b):
                pe.wait_ge(ctx_loaded, 16 * (b + 1))
                if b >= 3:
                    pe.wait_ge(base_ready, RT * (b - 2))
                if b:
                    pe.wait_ge(s1_done, 7 * b)
                for j in range(RT):
                    mm = nc.tensor.transpose(b_sim[0][:, j * P:(j + 1) * P], ctx_sb[:, j], ident[:, :])
                mm.then_inc(s1_ps, 1)
                pe.wait_ge(s1_done, 7 * b + 1)
                if b == 0:
                    pe.wait_ge(wT_ready, 1)
                if b >= 3:
                    pe.wait_ge(ht_done, RT * (b - 2))
                nc.tensor.matmul(b_sim[1][:, :], wqkT[:, 0], ctxT[:, :], start=True, stop=True).then_inc(s1_ps, 1)
                nc.tensor.matmul(b_sim[0][:, :], wqkT[:, 1], ctxT[:, :], start=True, stop=True).then_inc(s1_ps, 1)

            def stage1_out(b, i):
                pe.wait_ge(s1_done, 7 * b + 3)
                if i >= 2:
                    pe.wait_ge(s1_done, 7 * b + i + 2)
                nc.tensor.matmul(b_sim[(3 + i) % 2][:, :], qT[:, i * P:(i + 1) * P], kT[:, :],
                                 start=True, stop=True).then_inc(s1_ps, 1)

            def check_search(b):
                pe.wait_ge(bad_in, b + 1)
                nc.tensor.matmul(ps_bad, ones[:, 0:1], bad[:, :], start=True, stop=True).then_inc(bad_ps, 1)

            pe.wait_ge(scal_ready, 1)
            nc.tensor.matmul(b_small[:, 0:3], ones_f[0:1, :], scal_t[0:1, 0:3], start=True, stop=True).then_inc(gates_bc, 1)
            for b in range(2):
                stage1_in(b)
                for i in range(RT):
                    stage1_out(b, i)
            pe.wait_ge(gates_ready, 1)
            check_search(0)
            for b in range(B):
                q = b % 2
                pe.wait_ge(masked, RT * (b + 1))
                for i in range(RT):
                    if i < 2:
                        if b:
                            pe.wait_ge(x2t_done, RT * b)
                    else:
                        pe.wait_ge(at_used, RT * b + i - 1)
                    for j in range(RT):
                        nc.tensor.matmul(b_t[i % 2][:, j * P:(j + 1) * P], adj[:, q, j, i * P:(i + 1) * P], ident[:, :],
                                         start=(j == 0), stop=False, skip_group_check=True)
                    nc.tensor.matmul(b_t[i % 2][:, :], ident[:, :], adj[:, q, i], start=False, stop=True,
                                     skip_group_check=True).then_inc(at_ps, 1)
                if b + 2 < B:
                    stage1_in(b + 2)
                for i in range(RT):
                    pe.wait_ge(x2_ready, RT * b + i + 1)
                    if i < 2:
                        pe.wait_ge(at_used, RT * b + i + 3)
                    else:
                        pe.wait_ge(x2t_done, RT * b + i - 1)
                    for c in range(DC):
                        mm = nc.tensor.transpose(b_t[i % 2][:, c * P:(c + 1) * P], x2[:, i, c * P:(c + 1) * P], ident[:, :])
                    mm.then_inc(x2t_ps, 1)
                if b == 0:
                    pe.wait_ge(rtw_in, 16)
                for i in range(RT):
                    pe.wait_ge(x2t_done, RT * b + i + 1)
                    for c in range(DC):
                        mm = nc.tensor.matmul(ps_logit[:, i * E:(i + 1) * E], x2T[:, i, c], w_rt[:, c, :],
                                              start=(c == 0), stop=(c == DC - 1))
                mm.then_inc(logit_ps, 1)
                if b == 0:
                    pe.wait_ge(shw_in, 48)

                def up(i):
                    n = RT * b + i
                    if n >= 2:
                        pe.wait_ge(h_ready, n - 1)
                    for c in range(DC):
                        mm = nc.tensor.matmul(b_gu[n % 2][:, :], x2T[:, i, c], w_shgu[:, c, :],
                                              start=(c == 0), stop=(c == DC - 1))
                    mm.then_inc(gu_ps, 1)

                def down(i):
                    n = RT * b + i
                    pe.wait_ge(h_ready, n + 1)
                    if i == 0:
                        pe.wait_ge(s1_done, 7 * min(b + 3, B))
                    if n:
                        pe.wait_ge(ht_done, n)
                    for c in range(IC):
                        mm = nc.tensor.transpose(b_sim[1][:, c * P:(c + 1) * P], h[:, n % 2, c * P:(c + 1) * P], ident[:, :])
                    mm.then_inc(ht_ps, 1)
                    pe.wait_ge(ht_done, n + 1)
                    if n > 1:
                        pe.wait_ge(base_ready, n - 1)
                    for c in range(IC):
                        mm = nc.tensor.matmul(b_y[n % 2][:, :], hT[:, n % 2, c], w_shdn[:, c, :], start=(c == 0), stop=(c == IC - 1))
                    mm.then_inc(y_ps, 1)

                for i in range(2):
                    if b + 2 < B:
                        stage1_out(b + 2, 2 * i)
                        stage1_out(b + 2, 2 * i + 1)
                    up(i)
                pe.wait_ge(mask_ready, b + 1)
                if b:
                    pe.wait_ge(msum_ready, b)
                for i in range(RT):
                    dst = ps_rank[:, i * E:(i + 1) * E]
                    nc.tensor.matmul(dst, upper[:, :], mask[:, i], start=True, stop=False)
                    for j in range(i):
                        nc.tensor.matmul(dst, ones[:, :], mask[:, j], start=False, stop=False)
                    mm = nc.tensor.matmul(dst, ones[:, :], msum[:, :], start=False, stop=True)
                mm.then_inc(rank_ps, 1)
                for i in range(RT):
                    down(i)
                    if i + 2 < RT:
                        up(i + 2)
                    if i == 2 and b + 1 < B:
                        check_search(b + 1)

                pe.wait_ge(slot_oh, b + 1)
                if b:
                    pe.wait_ge(table_used, b)
                for n in range(2 * RT):
                    mm = nc.tensor.matmul(ps_table, oh_slot[:, n], oh_col[:, n].rearrange("p a c -> p (a c)"),
                                          start=(n == 0), stop=(n == 2 * RT - 1))
                mm.then_inc(table_ps, 1)

            pe.wait_ge(msum_ready, B)
            nc.tensor.matmul(b_t[0][0:E, 0:1], msum[:, :], ones[:, 0:1], start=True, stop=True).then_inc(fin_t, 1)
            pe.wait_ge(fin_v, 4)
            nc.tensor.matmul(b_t[1][:, 0:1], e_lt[:, :], tiles_b[:, :], start=True, stop=True)
            nc.tensor.matmul(b_t[1][:, 1:2], e_eq[:, :], tiles_b[:, :], start=True, stop=True).then_inc(fin_t, 1)
            pe.wait_ge(fin_v, FIN_V_TABLE)
            nc.tensor.transpose(b_gu[0][:, 0:COLS], table[:, 0], ident[:, :]).then_inc(fin_t, 1)
            pe.wait_ge(fin_v, FIN_V_PLACE)
            nc.tensor.matmul(b_gu[1][:, 0:MT], table_t, place, start=True, stop=True)
            nc.tensor.matmul(b_gu[1][:, 64:64 + MT], e_of[:, :], place, start=True, stop=True).then_inc(fin_t, 1)

            def transpose_in(t, par):
                pe.wait_ge(gathered[par], gather_count(t, par))
                for c in range(DC):
                    mm = nc.tensor.transpose(b_t[par][:, c * P:(c + 1) * P], xg[:, par, c * P:(c + 1) * P], ident[:, :])
                mm.then_inc(m_xt_ps, 1)

            def expert_of(t):
                return pe.value_load(etab[0:1, bass.ds(t, 1)], min_val=0, max_val=E - 1)

            def up_m(t, par):
                e = expert_of(t)
                pe.wait_ge(m_xt, t + 1)
                for c in range(DC):
                    mm = nc.tensor.matmul(b_gu[par][:, :], xgT[:, par, c], w_gu[:, bass.ds(e * (DC * F2) + c * F2, F2)],
                                          start=(c == 0), stop=(c == DC - 1))
                mm.then_inc(m_gu_ps, 1)

            def turn_h(t, par):
                pe.wait_ge(m_h, t + 1)
                for c in range(IC):
                    mm = nc.tensor.transpose(bank[par][:, c * P:(c + 1) * P], h[:, par, c * P:(c + 1) * P], ident[:, :])
                mm.then_inc(m_ht_ps, 1)

            def down_m(t, par):
                e = expert_of(t)
                pe.wait_ge(m_ht, t + 1)
                if not (isinstance(t, int) and t < 2):
                    pe.wait_ge(m_y, t - 1)
                for c in range(IC):
                    mm = nc.tensor.matmul(b_sim[par][:, :], hT[:, par, c], w_dn[:, bass.ds(e * (IC * D) + c * D, D)],
                                          start=(c == 0), stop=(c == IC - 1))
                mm.then_inc(m_y_ps, 1)

            def step(t, par, last=False):
                turn_h(t - 1, 1 - par)
                if not last:
                    transpose_in(t + 1, 1 - par)
                up_m(t, par)
                down_m(t - 1, 1 - par)

            pe.wait_ge(exw_in, 2 * 16 * E)
            pe.wait_ge(fin_v, FIN_V_IDX)
            transpose_in(0, 0)
            transpose_in(1, 1)
            up_m(0, 0)
            step(1, 1)
            step(2, 0)
            with pe.Fori(3, MT - 3, 2) as t:
                step(t, 1)
                step(t + 1, 0)
            step(MT - 2, 1)
            step(MT - 1, 0, True)
            turn_h(MT - 1, 0)
            down_m(MT - 1, 0)

        @block.vector
        def _(dve):
            steps = [0]
            V = nc.vector

            def link(ins):
                steps[0] += 1
                ins.then_inc(vector_step, 1)
                dve.wait_ge(vector_step, steps[0])

            dve.wait_ge(const_ready, 1)

            def split_partitions():
                link(V.tensor_scalar(part_i[:, 1:2], part_i[:, 0:1], CAP.bit_length() - 1, None, ALU.logical_shift_right))
                link(V.tensor_scalar(part_i[:, 2:3], part_i[:, 0:1], CAP - 1, None, ALU.bitwise_and))
                link(V.tensor_copy(r_of[:, :], part_i[:, 2:3]))
                link(V.tensor_copy(e_of[:, :], part_i[:, 1:2].to_broadcast([P, P])))

            def x_stats(b):
                q = b % 2
                dve.wait_ge(x_in[q], 16 * (b // 2 + 1))
                for i in range(RT):
                    ins = V.bn_stats(stats[:, i], xs[:, q, i])
                link(ins)
                for i in range(RT):
                    ins = V.bn_aggr(mv[:, i], stats[:, i])
                link(ins)

            def start_search(b):
                q = b % 2
                dve.wait_ge(s1_done, 7 * (b + 1))
                link(V.tensor_scalar(mean[:, :], simsum[:, q], 1.0 / N, None, ALU.mult))
                link(V.tensor_tensor(msq[:, :], mean[:, :], mean[:, :], ALU.mult))
                link(V.scalar_tensor_tensor(powin[:, 0], simsq[:, q], 1.0 / N, msq[:, :], ALU.mult, ALU.subtract))
                link(V.tensor_scalar(powin[:, 0], powin[:, 0], 1e-30, None, ALU.max))
                V.tensor_scalar(powin[:, 1], mv[:, :, 1], EPS, None, ALU.add).then_inc(pow_in, 1)
                dve.wait_ge(pow_out, b + 1)
                V.scalar_tensor_tensor(probe[:, 0], powout[:, 0], Z_START, mean[:, :], ALU.mult,
                                       ALU.add).then_inc(probe_ready, 1)
                link(V.tensor_scalar(xmul[:, :], powout[:, 1], c12[:, 0:1], None, ALU.mult))
                V.tensor_copy(dev[:, :], powout[:, 0])
                link(V.scalar_tensor_tensor(xadd[:, :], mv[:, :, 0], -1.0, xmul[:, :], ALU.mult, ALU.mult))
                V.tensor_scalar(xmul[:, :], xmul[:, :], 1.0, None, ALU.add).then_inc(affine_in, 1)

            def count(b, k):
                if k == 0:
                    dve.wait_ge(probe_ready, (COUNTS - 1) * b + 1)
                for i in range(RT if k == COUNTS - 1 else SHARE):
                    ins = V.tensor_scalar(ge[:, i], sim[:, b % 2, i], probe[:, k, i:i + 1], None, ALU.is_ge, ALU.add,
                                          accum_out=cnt[:, k, i:i + 1])
                link(ins)

            def move(b, k):
                dve.wait_ge(sign_ready, (COUNTS - 1) * b + k + 1)
                V.tensor_scalar(err[:, k, SHARE:RT], sgn[:, k, SHARE:RT], -0.5, N / 2 - AIM, ALU.mult, ALU.add)
                link(V.tensor_scalar(err[:, k, 0:SHARE], cnt[:, k, 0:SHARE], AIM, None, ALU.subtract))
                V.tensor_tensor(u[:, 0], err[:, k], err[:, k], ALU.mult)
                if k:
                    link(V.tensor_tensor(u[:, 2], err[:, k - 1], err[:, k], ALU.subtract))
                    V.scalar_tensor_tensor(u[:, 1], u[:, 0], DONE, err[:, k], ALU.is_gt, ALU.mult)
                    V.tensor_tensor(u[:, 3], u[:, 2], dz[:, k - 1], ALU.mult)
                    link(V.tensor_tensor(u[:, 2], u[:, 2], u[:, 2], ALU.mult))
                    link(V.tensor_scalar(u[:, 2], u[:, 2], 0.25, None, ALU.max))
                    link(V.reciprocal(u[:, 2], u[:, 2]))
                    link(V.tensor_tensor(u[:, 3], u[:, 3], u[:, 2], ALU.mult))
                    link(V.tensor_scalar(u[:, 3], u[:, 3], 0.4 / DENS, 4.0 / DENS, ALU.max, ALU.min))
                    link(V.tensor_tensor(dz[:, k], u[:, 3], u[:, 1], ALU.mult))
                else:
                    link(V.tensor_scalar(u[:, 3], err[:, k], 1.0 / DENS, None, ALU.mult))
                    link(V.scalar_tensor_tensor(dz[:, k], u[:, 0], DONE, u[:, 3], ALU.is_gt, ALU.mult))
                link(V.tensor_tensor(u[:, 4], dz[:, k], dev[:, :], ALU.mult))
                if k + 1 < COUNTS - 1:
                    V.tensor_tensor(probe[:, k + 1], probe[:, k], u[:, 4], ALU.add).then_inc(probe_ready, 1)
                    dve.wait_ge(probe_ready, (COUNTS - 1) * b + k + 2)
                else:
                    link(V.tensor_tensor(probe[:, k + 1], probe[:, k], u[:, 4], ALU.add))

            def finish_search(b):
                q, k = b % 2, COUNTS - 1
                V.tensor_scalar(u[:, 6], cnt[:, k], -1.0, float(KTH - 1), ALU.mult, ALU.add)
                V.tensor_scalar(u[:, 0], cnt[:, k], float(KTH), None, ALU.is_ge)
                link(V.tensor_scalar(u[:, 1], cnt[:, k], float(KTH - WIN), None, ALU.is_lt))
                V.tensor_tensor(bad[:, :], u[:, 0], u[:, 1], ALU.add).then_inc(bad_in, 1)
                for j in range(0, RT, 2):
                    for i in (j, j + 1):
                        if j:
                            dve.wait_ge(top8_ready, RT * b + i - 1)
                        V.scalar_tensor_tensor(tmp[:, i % 2], ge[:, i], -BIG, sim[:, q, i], ALU.mult,
                                               ALU.add).then_inc(below_ready, 1)
                    for i in (j, j + 1):
                        dve.wait_ge(below_ready, RT * b + i + 1)
                        V.max(top8[:, i], tmp[:, i % 2]).then_inc(top8_ready, 1)
                dve.wait_ge(top8_ready, RT * (b + 1))
                for i in range(RT):
                    ins = V.scalar_tensor_tensor(sel8[:, i], iota8[:, :], u[:, 6, i:i + 1], top8[:, i],
                                                 ALU.is_equal, ALU.mult, accum_out=thr[:, i:i + 1])
                link(ins)
                dve.wait_ge(bad_ps, b + 1)
                V.tensor_copy(bad_i[:, 0:RT], ps_bad)
                link(V.tensor_reduce(bad_f[:, :], ps_bad, AX_X, ALU.add))
                link(V.tensor_copy(bad_i[:, RT:RT + 1], bad_f[:, :]))
                unfinished = dve.value_load(bad_i[0:1, RT:RT + 1])
                with dve.If(unfinished > 0):
                    for i in range(RT):
                        unfinished_tile = dve.value_load(bad_i[0:1, i:i + 1])
                        with dve.If(unfinished_tile > 0):
                            V.tensor_copy(tmp[:, 0], sim[:, q, i])
                            dve.drain()
                            with dve.Fori(0, (KTH - 1) // WIN) as _:
                                V.max(top8[:, i], tmp[:, 0])
                                dve.drain()
                                V.match_replace(tmp[:, 0], top8[:, i], tmp[:, 0], -3e38)
                                dve.drain()
                            V.max(top8[:, i], tmp[:, 0])
                            dve.drain()
                            V.tensor_copy(thr[:, i:i + 1], top8[:, i, (KTH - 1) % WIN:(KTH - 1) % WIN + 1])
                            dve.drain()

            def mask_adjacency(b):
                q = b % 2
                for i in range(RT):
                    V.scalar_tensor_tensor(adj[:, q, i], sim[:, q, i], thr[:, i:i + 1], adj[:, q, i],
                                           ALU.is_ge, ALU.mult).then_inc(masked, 1)

            def add_adjacency(b):
                q = b % 2
                dve.wait_ge(affine_out, RT * (b + 1))
                dve.wait_ge(masked, RT * (b + 1))
                for i in range(RT):
                    dve.wait_ge(at_ps, RT * b + i + 1)
                    V.scalar_tensor_tensor(xs[:, q, i], b_t[i % 2][:, :], c12[:, 1:2], xs[:, q, i], ALU.mult,
                                           ALU.add).then_inc(at_used, 1)
                    if i:
                        dve.wait_ge(at_used, RT * b + i)
                        V.bn_stats(stats[:, i - 1], xs[:, q, i - 1])
                dve.wait_ge(at_used, RT * (b + 1))
                link(V.bn_stats(stats[:, RT - 1], xs[:, q, RT - 1]))
                for i in range(RT):
                    ins = V.bn_aggr(mv[:, i], stats[:, i])
                link(ins)
                if b:
                    dve.wait_ge(x2_ready, RT * b)
                V.tensor_scalar(pow2in[:, :], mv[:, :, 1], EPS, None, ALU.add).then_inc(pow2_in, 1)
                dve.wait_ge(pow2_out, b + 1)
                V.scalar_tensor_tensor(x2add[:, :], mv[:, :, 0], -1.0, pow2out[:, :], ALU.mult, ALU.mult).then_inc(x2_in, 1)

            def pick_experts(b):
                dve.wait_ge(logit_ps, b + 1)
                if b:
                    dve.wait_ge(prob_ready, b)
                V.tensor_copy(logit[:, :, :], ps_logit.rearrange("p (i e) -> p i e", e=E)).then_inc(logit_used, 1)
                dve.wait_ge(logit_used, b + 1)
                for i in range(RT):
                    ins = V.max(v8[:, i], logit[:, i])
                link(ins)
                for i in range(RT):
                    ins = V.max_index(i8[:, i], v8[:, i], logit[:, i])
                ins.then_inc(top2, 1)
                dve.wait_ge(top2, b + 1)
                link(V.tensor_copy(ef[:, :, :], i8[:, :, 0:2].rearrange("p i k -> p k i")))
                for k in range(2):
                    ins = V.tensor_tensor(oh[:, k], ef[:, k].unsqueeze(2).to_broadcast([P, RT, E]),
                                          iota8[:, :].unsqueeze(1).to_broadcast([P, RT, E]), ALU.is_equal)
                link(ins)
                V.tensor_tensor(mask[:, :, :], oh[:, 0], oh[:, 1], ALU.add).then_inc(mask_ready, 1)

            def weigh_experts(b):
                dve.wait_ge(prob_ready, b + 1)
                for k in range(2):
                    ins = V.tensor_tensor(ohp[:, k], oh[:, k], prob[:, :, k].unsqueeze(2).to_broadcast([P, RT, E]), ALU.mult)
                link(ins)
                if b:
                    dve.wait_ge(rows_out, 16 * b)
                V.tensor_tensor(x2[:, :, D:ROW], ohp[:, 0], ohp[:, 1], ALU.add).then_inc(payload, 1)

            def rank_tokens(b):
                dve.wait_ge(rank_ps, b + 1)
                for k in range(2):
                    ins = V.tensor_tensor(rsel[:, k].rearrange("p i e -> p (i e)"), oh[:, k].rearrange("p i e -> p (i e)"),
                                          ps_rank, ALU.mult)
                link(ins)
                link(V.tensor_reduce(rank[:, :], rsel[:, :, :, :].rearrange("p k i e -> p (k i) e"), AX_X, ALU.add))
                link(V.tensor_reduce(mred[:, :], mask[:, :, :].rearrange("p i e -> p e i"), AX_X, ALU.add))
                V.tensor_tensor(msum[:, :], msum[:, :], mred[:, :], ALU.add).then_inc(msum_ready, 1)
                link(V.tensor_copy(rank_i[:, 0], rank[:, :]))
                V.tensor_scalar(rank_i[:, 1], rank_i[:, 0], P.bit_length() - 1, None, ALU.logical_shift_right)
                link(V.tensor_scalar(rank_i[:, 2], rank_i[:, 0], P - 1, None, ALU.bitwise_and))
                if b:
                    dve.wait_ge(slot_oh, b)
                link(V.tensor_copy(rank_f[:, :, :], rank_i[:, 1:3]))
                V.scalar_tensor_tensor(col[:, :], ef[:, :, :].rearrange("p k i -> p (k i)"), float(CAP), rank_f[:, 0],
                                       ALU.mult, ALU.add)
                V.scalar_tensor_tensor(delta[:, :], rank_f[:, 1], -1.0, part[:, 0:1].to_broadcast([P, 2 * RT]),
                                       ALU.mult, ALU.add).then_inc(slot_known, 1)

            def one_hots():
                dve.wait_ge(slot_known, B)
                dve.wait_ge(table_ps, B - 1)
                for n in range(2 * RT):
                    tile = float(RT * (B - 1) + n % RT - CAP)
                    V.tensor_scalar(oh_slot[:, n], iota_b[:, :], rank_f[:, 1, n:n + 1], None, ALU.is_equal)
                    V.tensor_scalar(oh_col[:, n, 0], iota_b[:, :], col[:, n:n + 1], tile, ALU.is_equal, ALU.mult)
                    ins = V.tensor_scalar(oh_col[:, n, 1], iota_b[:, :], col[:, n:n + 1], delta[:, n:n + 1],
                                          ALU.is_equal, ALU.mult)
                ins.then_inc(slot_oh, 1)

            def gate_hidden(b, i):
                n = RT * b + i
                dve.wait_ge(silu_ready, n + 1)
                if n >= 2:
                    dve.wait_ge(ht_ps, n - 1)
                V.tensor_tensor(h[:, n % 2], b_gu[n % 2][:, I:F2], silu[:, n % 2], ALU.mult).then_inc(h_ready, 1)

            def make_base(b, i):
                n = RT * b + i
                dve.wait_ge(y_ps, n + 1)
                V.scalar_tensor_tensor(xs[:, b % 2, i], b_y[n % 2][:, :], gates[:, 1:2], xs[:, b % 2, i],
                                       ALU.mult, ALU.add).then_inc(base_ready, 1)

            def keep_table(b):
                dve.wait_ge(table_ps, b + 1)
                dst = table[:, :, :].rearrange("p a c -> p (a c)")
                if b == 0:
                    V.tensor_copy(dst, ps_table).then_inc(table_used, 1)
                else:
                    V.tensor_tensor(dst, dst, ps_table, ALU.add).then_inc(table_used, 1)
                dve.wait_ge(table_used, b + 1)

            split_partitions()
            dve.wait_ge(gates_ready, 1)
            link(V.tensor_tensor(c12[:, 2:3], gates[:, 2:3], gates[:, 0:1], ALU.mult))
            link(V.tensor_tensor(c12[:, 0:1], gates[:, 0:1], c12[:, 2:3], ALU.subtract))
            link(V.tensor_scalar(c12[:, 1:2], c12[:, 2:3], 0.5, None, ALU.mult))
            x_stats(0)
            start_search(0)
            for k in range(COUNTS - 1):
                count(0, k)
                move(0, k)
            count(0, COUNTS - 1)
            finish_search(0)
            mask_adjacency(0)
            add_adjacency(0)
            for b in range(B):
                more = b + 1 < B
                if more:
                    x_stats(b + 1)
                    start_search(b + 1)
                    for k in range(2):
                        count(b + 1, k)
                        move(b + 1, k)
                pick_experts(b)
                if more:
                    count(b + 1, 2)
                    move(b + 1, 2)
                    count(b + 1, 3)
                gate_hidden(b, 0)
                rank_tokens(b)
                if not more:
                    one_hots()
                gate_hidden(b, 1)
                weigh_experts(b)
                if more:
                    move(b + 1, 3)
                gate_hidden(b, 2)
                make_base(b, 0)
                if more:
                    count(b + 1, COUNTS - 1)
                gate_hidden(b, 3)
                make_base(b, 1)
                if more:
                    finish_search(b + 1)
                    mask_adjacency(b + 1)
                make_base(b, 2)
                make_base(b, 3)
                keep_table(b)
                if more:
                    add_adjacency(b + 1)

            done = [0]

            def fin(ins):
                done[0] += 1
                ins.then_inc(fin_v, 1)
                dve.wait_ge(fin_v, done[0])

            dve.wait_ge(fin_t, 1)
            fin(V.tensor_copy(n_e[:, 0:1], b_t[0][0:E, 0:1]))
            fin(V.tensor_scalar(tiles_e[:, 1:2], b_t[0][0:E, 0:1], float(P - 1), None, ALU.add))
            fin(V.tensor_copy(n_e[:, 0:1], tiles_e[:, 1:2]))
            link(V.tensor_scalar(n_e[:, 1:2], n_e[:, 0:1], P.bit_length() - 1, None, ALU.logical_shift_right))
            fin(V.tensor_copy(tiles_b[:, :], n_e[:, 1:2]))
            fin(V.scalar_tensor_tensor(table[:, 0], table[:, 0], float(P), table[:, 1], ALU.mult, ALU.add))
            assert done[0] == FIN_V_TABLE
            dve.wait_ge(fin_t, 2)
            link(V.tensor_copy(tile_pos[:, 0:2], b_t[1][:, 0:2]))
            link(V.tensor_tensor(tile_pos[:, 1:2], tile_pos[:, 1:2], r_of[:, :], ALU.is_gt))
            link(V.tensor_tensor(tile_pos[:, 0:1], tile_pos[:, 0:1], r_of[:, :], ALU.add))
            link(V.scalar_tensor_tensor(tile_pos[:, 2:3], tile_pos[:, 0:1], 1.0, tile_pos[:, 1:2], ALU.add, ALU.mult))
            link(V.tensor_scalar(tile_pos[:, 3:4], tile_pos[:, 2:3], 1.0, None, ALU.subtract))
            link(V.tensor_scalar(place, iota_m[:, :], tile_pos[:, 3:4], None, ALU.is_equal))
            dve.wait_ge(fin_t, 3)
            fin(V.tensor_copy(table_t, b_gu[0][:, 0:COLS]))
            assert done[0] == FIN_V_PLACE
            dve.wait_ge(fin_t, 4)
            V.tensor_scalar(idx[:, :], b_gu[1][:, 0:MT], part[:, 0:1], float(T), ALU.add, ALU.add)
            V.tensor_copy(etab[:, :], b_gu[1][0:1, 64:64 + MT])
            fin(V.tensor_tensor(oh_e, b_gu[1][:, 64:64 + MT].unsqueeze(2).to_broadcast([P, MT, E]),
                                iota8[:, :].unsqueeze(1).to_broadcast([P, MT, E]), ALU.is_equal))
            assert done[0] == FIN_V_IDX

            def weight_of(t, par):
                dve.wait_ge(gathered[par], gather_count(t, par))
                V.scalar_tensor_tensor(p_junk[:, par], xg[:, par, D:ROW], 1.0, adj[:, 0, 1, bass.ds(t * E, E)],
                                       ALU.mult, ALU.mult, accum_out=p_t[:, par:par + 1]).then_inc(m_p, 1)

            def gate(t, par):
                dve.wait_ge(m_silu, t + 1)
                dve.wait_ge(m_p, t + 1)
                V.scalar_tensor_tensor(h[:, par], b_gu[par][:, I:F2], p_t[:, par:par + 1], silu[:, par],
                                       ALU.mult, ALU.mult).then_inc(m_h, 1)

            def ht_out(t, par):
                dve.wait_ge(m_ht_ps, t + 1)
                V.tensor_copy(hT[:, par], bank[par][:, 0:I].rearrange("p (c t) -> p c t", c=IC)).then_inc(m_ht, 1)

            def step(t, par, last=False):
                if not (isinstance(t, int) and t < 3):
                    dve.wait_ge(m_y_ps, t - 2)
                ht_out(t - 1, 1 - par)
                if not last:
                    weight_of(t + 1, 1 - par)
                gate(t, par)

            weight_of(0, 0)
            weight_of(1, 1)
            gate(0, 0)
            step(1, 1)
            step(2, 0)
            with dve.Fori(3, MT - 3, 2) as t:
                step(t, 1)
                step(t + 1, 0)
            step(MT - 2, 1)
            step(MT - 1, 0, True)
            dve.wait_ge(m_y_ps, MT - 2)
            ht_out(MT - 1, 0)


FIN_V_TABLE, FIN_V_PLACE, FIN_V_IDX = 5, 6, 7


def gather_count(t, par):
    return 8 * t + (8 if par else 16)


_INS = ["x", "ctx_512", "g_xattn", "g_ffn", "L0_xattn_Wq", "L0_xattn_Wk", "L0_xattn_gamma_raw", "L0_ffn_router_w",
        "L0_ffn_gate_up_w", "L0_ffn_down_w", "L0_ffn_shared_gate_w", "L0_ffn_shared_up_w", "L0_ffn_shared_down_w"]


def kernel(**inputs):
    import numpy as _np
    import concourse.bacc as _bacc
    from concourse import mybir as _mybir
    from concourse.bass_utils import run_bass_kernel_spmd as _run

    nc = _bacc.Bacc("TRN2", target_bir_lowering=False, num_devices=1)
    arrays, args = {}, []
    for name in _INS:
        a = _np.ascontiguousarray(inputs[name])
        if a.size == 1:
            a = a.reshape(1, 1)
        arrays[f"in_{name}_dram"] = a
        args.append(nc.dram_tensor(f"in_{name}_dram", a.shape, _mybir.dt.from_np(a.dtype), kind="ExternalInput").ap())
    b, n, d = inputs["x"].shape
    out = nc.dram_tensor("out_dram", (b * n + 128, d), _mybir.dt.from_np(_np.dtype("float32")), kind="ExternalOutput").ap()
    flamingo_gated_block(nc, *args, out)
    r = _run(nc, [arrays], core_ids=[0])
    return r.results[0]["out_dram"][:b * n].reshape(b, n, d)
```
